# Optimizing a Trainium2 kernel written in Bass

```python
import numpy as np
import jax
import jax.numpy as jnp

def _softmax(x, axis=-1):
    return jax.nn.softmax(x, axis=axis)

def _gelu(x):
    return jax.nn.gelu(x, approximate=True)

def _silu(x):
    return jax.nn.silu(x)

def _sigmoid(x):
    return jax.nn.sigmoid(x)

def _layernorm(x, axis=-1, eps=1e-05):
    m = jnp.mean(x, axis=axis, keepdims=True)
    v = jnp.var(x, axis=axis, keepdims=True)
    return (x - m) / jnp.sqrt(v + eps)

def _scatter_add(tgt, idx, src, axis=0):
    return tgt.at[idx].add(src)

def _segment_sum(src, seg, n):
    return jax.ops.segment_sum(src, seg, n)
kernel_name = 'mk_metaformer_d1_conv_nhwc384_r4_028075'

def setup_inputs(seed: int=0):
    np.random.seed(seed)
    _w = jnp.asarray

    def _rec_inputs():
        import jax
        import jax.numpy as jnp
        _gk = jax.random.key(seed)
        x = -0.0001476 + 0.9999 * jax.random.normal(jax.random.fold_in(_gk, 1), (32, 56, 56, 96), jnp.float32)
        return x
    x = _rec_inputs()

    def _L0_conv_setup():
        import math
        import jax, jax.numpy as jnp
        import numpy as np
        W_SIZE = 7
        NUM_HEADS = 12

        def _shift_masks(w: int, d: int):
            ul = np.zeros((w * w, w * w), np.float32)
            ul[-d * w:, :-d * w] = -np.inf
            ul[:-d * w, -d * w:] = -np.inf
            lr = np.zeros((w, w, w, w), np.float32)
            lr[:, -d:, :, :-d] = -np.inf
            lr[:, :-d, :, -d:] = -np.inf
            lr = lr.reshape(w * w, w * w)
            return (jnp.asarray(ul), jnp.asarray(lr))

        def _rel_pos_index(w: int):
            coords = np.stack(np.meshgrid(np.arange(w), np.arange(w), indexing='ij'), 0).reshape(2, -1)
            rel = coords[:, :, None] - coords[:, None, :]
            idx = (rel[0] + w - 1) * (2 * w - 1) + (rel[1] + w - 1)
            return jnp.asarray(idx, dtype=jnp.int32)
        key = jax.random.key(seed)
        ks = jax.random.split(key, 6)
        E, w = (96, W_SIZE)
        return {'x': jax.random.normal(ks[0], (32, 56, 56, E), jnp.float32), 'w_qkv': jax.random.normal(ks[1], (3 * E, E), jnp.float32) * 0.02, 'b_qkv': jax.random.normal(ks[2], (3 * E,), jnp.float32) * 0.02, 'w_proj': jax.random.normal(ks[3], (E, E), jnp.float32) * 0.02, 'b_proj': jax.random.normal(ks[4], (E,), jnp.float32) * 0.02, 'rel_table': jax.random.normal(ks[5], ((2 * w - 1) ** 2, NUM_HEADS), jnp.float32) * 0.02}
    _L0_conv_all = _L0_conv_setup()
    _L0_conv_in = {k: v for k, v in _L0_conv_all.items() if k in ('w_qkv', 'b_qkv', 'w_proj', 'b_proj', 'rel_table')}
    del _L0_conv_all

    def _L0_ffn_setup():
        import jax, jax.numpy as jnp
        import numpy as np
        NUM_EXPERTS = 4
        TOP_K = 2
        DIM = 96
        HID = 4 * DIM
        key = jax.random.key(seed)
        ks = jax.random.split(key, 5)
        B, S = (16, 512)
        scale_in = 1.0 / np.sqrt(DIM)
        scale_hid = 1.0 / np.sqrt(HID)
        return {'x': jax.random.normal(ks[0], (B, S, DIM), dtype=jnp.float32), 'gate_w': jax.random.normal(ks[1], (DIM, NUM_EXPERTS), dtype=jnp.float32) * scale_in, 'gate_b': jnp.zeros((NUM_EXPERTS,), dtype=jnp.float32), 'w1': jax.random.normal(ks[2], (NUM_EXPERTS, DIM, HID), dtype=jnp.float32) * scale_in, 'b1': jnp.zeros((NUM_EXPERTS, HID), dtype=jnp.float32), 'w2': jax.random.normal(ks[3], (NUM_EXPERTS, HID, DIM), dtype=jnp.float32) * scale_hid, 'b2': jnp.zeros((NUM_EXPERTS, DIM), dtype=jnp.float32)}
    _L0_ffn_all = _L0_ffn_setup()
    _L0_ffn_in = {k: v for k, v in _L0_ffn_all.items() if k in ('gate_w', 'gate_b', 'w1', 'b1', 'w2', 'b2')}
    del _L0_ffn_all
    return {'x': x, 'L0_conv_w_qkv': _L0_conv_in['w_qkv'], 'L0_conv_b_qkv': _L0_conv_in['b_qkv'], 'L0_conv_w_proj': _L0_conv_in['w_proj'], 'L0_conv_b_proj': _L0_conv_in['b_proj'], 'L0_conv_rel_table': _L0_conv_in['rel_table'], 'L0_ffn_gate_w': _L0_ffn_in['gate_w'], 'L0_ffn_gate_b': _L0_ffn_in['gate_b'], 'L0_ffn_w1': _L0_ffn_in['w1'], 'L0_ffn_b1': _L0_ffn_in['b1'], 'L0_ffn_w2': _L0_ffn_in['w2'], 'L0_ffn_b2': _L0_ffn_in['b2']}

def reference(x, L0_conv_w_qkv, L0_conv_b_qkv, L0_conv_w_proj, L0_conv_b_proj, L0_conv_rel_table, L0_ffn_gate_w, L0_ffn_gate_b, L0_ffn_w1, L0_ffn_b1, L0_ffn_w2, L0_ffn_b2):
    import jax
    import jax.numpy as jnp

    def _L0_conv_ref(x, w_qkv, b_qkv, w_proj, b_proj, rel_table):
        import math
        import jax, jax.numpy as jnp
        import numpy as np
        W_SIZE = 7
        NUM_HEADS = 12

        def _shift_masks(w: int, d: int):
            ul = np.zeros((w * w, w * w), np.float32)
            ul[-d * w:, :-d * w] = -np.inf
            ul[:-d * w, -d * w:] = -np.inf
            lr = np.zeros((w, w, w, w), np.float32)
            lr[:, -d:, :, :-d] = -np.inf
            lr[:, :-d, :, -d:] = -np.inf
            lr = lr.reshape(w * w, w * w)
            return (jnp.asarray(ul), jnp.asarray(lr))

        def _rel_pos_index(w: int):
            coords = np.stack(np.meshgrid(np.arange(w), np.arange(w), indexing='ij'), 0).reshape(2, -1)
            rel = coords[:, :, None] - coords[:, None, :]
            idx = (rel[0] + w - 1) * (2 * w - 1) + (rel[1] + w - 1)
            return jnp.asarray(idx, dtype=jnp.int32)
        w = W_SIZE
        heads = NUM_HEADS
        B, H, Wd, C = x.shape
        hd = C // heads
        nh, nw, ww = (H // w, Wd // w, w * w)
        x = jnp.roll(x, (-w // 2, -w // 2), axis=(1, 2))
        xw = x.reshape(B, nh, w, nw, w, C).transpose(0, 1, 3, 2, 4, 5).reshape(B, nh, nw, ww, C)
        qkv = xw @ w_qkv.T + b_qkv
        q, k, v = jnp.split(qkv, 3, axis=-1)

        def heads_first(t):
            return t.reshape(B, nh, nw, ww, heads, hd).transpose(0, 1, 2, 4, 3, 5)
        q, k, v = (heads_first(q), heads_first(k), heads_first(v))
        attn = jnp.einsum('bhwnqd,bhwnkd->bhwnqk', q, k) * (1.0 / math.sqrt(hd))
        bias = rel_table[_rel_pos_index(w)].transpose(2, 0, 1)
        attn = attn + bias
        ul, lr = _shift_masks(w, w // 2)
        mask = jnp.zeros((nh, nw, 1, ww, ww), attn.dtype)
        mask = mask.at[-1].add(ul)
        mask = mask.at[:, -1].add(lr)
        attn = attn + mask
        p = jax.nn.softmax(attn, axis=-1)
        o = jnp.einsum('bhwnqk,bhwnkd->bhwnqd', p, v)
        o = o.transpose(0, 1, 2, 4, 3, 5).reshape(B, nh, nw, w, w, C)
        o = o.transpose(0, 1, 3, 2, 4, 5).reshape(B, H, Wd, C)
        o = jnp.roll(o, (w // 2, w // 2), axis=(1, 2))
        return o @ w_proj.T + b_proj

    def _L0_ffn_ref(x, gate_w, gate_b, w1, b1, w2, b2):
        import jax, jax.numpy as jnp
        import numpy as np
        NUM_EXPERTS = 4
        TOP_K = 2
        DIM = 96
        HID = 4 * DIM
        scores = jnp.einsum('bsd,de->bse', x, gate_w) + gate_b
        probs = jax.nn.softmax(scores, axis=-1)
        topk_vals, topk_idx = jax.lax.top_k(probs, TOP_K)
        mask = jnp.sum(jax.nn.one_hot(topk_idx, NUM_EXPERTS, dtype=probs.dtype), axis=-2)
        masked = probs * mask
        masked = masked / (jnp.sum(masked, axis=-1, keepdims=True) + 1e-09)
        h = jax.nn.gelu(jnp.einsum('bsd,edh->ebsh', x, w1) + b1[:, None, None, :], approximate=False)
        y = jnp.einsum('ebsh,ehd->ebsd', h, w2) + b2[:, None, None, :]
        out = jnp.einsum('bse,ebsd->bsd', masked, y)
        return out

    def _gn(v, G=32, eps=1e-05):
        B_, H_, W_, C_ = v.shape
        g = v.reshape(B_, H_, W_, G, C_ // G)
        m = jnp.mean(g, axis=(1, 2, 4), keepdims=True)
        s = jnp.var(g, axis=(1, 2, 4), keepdims=True)
        return ((g - m) / jnp.sqrt(s + eps)).reshape(v.shape)

    def _ln_c(v, eps=1e-06):
        m = jnp.mean(v, axis=-1, keepdims=True)
        s = jnp.var(v, axis=-1, keepdims=True)
        return (v - m) / jnp.sqrt(s + eps)

    def _ln_t(v, eps=1e-05):
        m = jnp.mean(v, axis=-1, keepdims=True)
        s = jnp.var(v, axis=-1, keepdims=True)
        return (v - m) / jnp.sqrt(s + eps)

    def _to_tokens(v):
        B_, H_, W_, C_ = v.shape
        return v.reshape(B_, H_ * W_, C_)

    def _from_tokens(t, like):
        return t.reshape(like.shape)
    x = x + _L0_conv_ref(_ln_c(x), L0_conv_w_qkv, L0_conv_b_qkv, L0_conv_w_proj, L0_conv_b_proj, L0_conv_rel_table)
    t = _to_tokens(x)
    t = t + _L0_ffn_ref(_ln_t(t), L0_ffn_gate_w, L0_ffn_gate_b, L0_ffn_w1, L0_ffn_b1, L0_ffn_w2, L0_ffn_b2)
    x = _from_tokens(t, x)
    return x

_drawn_inputs = setup_inputs


def setup_inputs(seed=0):
    import zlib

    import numpy as np

    out = dict(_drawn_inputs(seed))
    spreads = {'L0_ffn_gate_b': (0.0, 0.1), 'L0_ffn_b1': (0.0, 0.1), 'L0_ffn_b2': (0.0, 0.1)}
    factors = {'L0_conv_w_qkv': 3.24,
     'L0_conv_b_qkv': 4.046,
     'L0_conv_w_proj': 3.077,
     'L0_conv_rel_table': 8.0}
    for name, (base, spread) in spreads.items():
        noise = np.random.default_rng([zlib.crc32(name.encode()), seed]).standard_normal(out[name].shape)
        drawn = base * np.exp(spread * noise) if base else spread * noise
        out[name] = jnp.asarray(drawn.astype(out[name].dtype))
    for name, factor in factors.items():
        out[name] = (out[name] * factor).astype(out[name].dtype)
    return out
```

```python
from contextlib import ExitStack

import numpy as np

import concourse.bass as bass
from concourse import mybir

F32 = mybir.dt.float32
F16 = mybir.dt.float16
ALU = mybir.AluOpType
ACT = mybir.ActivationFunctionType
AX = mybir.AxisListType

B, IMG, C = 32, 56, 96
W = 7
WW = W * W
NW = IMG // W
HEADS, HD = 12, 8
PAIRS = HEADS // 2
GROUPS, GH = 3, 4
EXPERTS, HID = 4, 384
CHUNKS = EXPERTS * HID // 128
CPE = HID // 128
UPI = 4
UNITS = B * UPI
STRIP = W * IMG
TOK = 2 * STRIP
LANES = 2 * IMG
NB = 64
SPAN = NB + WW
SHIFT_IN, SHIFT_OUT = 4, 3
WSCALE = 64.0
EPS_C, EPS_T = 1e-6, 1e-5
ONES_ROW = 96
MASKED = -60000.0


def at(unit, per_unit, k=0):
    m, c = unit
    return m * (UPI * per_unit) + (c * per_unit + k)


def first(unit):
    return isinstance(unit[0], int) and unit == (0, 0)


def last(unit):
    return isinstance(unit[0], int) and unit == (B - 1, UPI - 1)


def piece_list(u, shift):
    out = []
    for half in range(2):
        c0 = (half * IMG // 2 + u * W + shift)
        runs = []
        n0 = min(W, max(0, IMG - c0))
        if n0:
            runs.append((0, n0, c0))
        if n0 < W:
            runs.append((n0, W - n0, (c0 + n0) % IMG))
        for r0, rows, row in ((0, IMG - shift, shift), (IMG - shift, shift, 0)):
            for cell, cols, col in runs:
                out.append((half * IMG + r0, rows, row, cell, cols, col))
    return out


N_T1, N_QK, N_V, N_S, N_PT, N_O = 2, 12, 2, 8, 16, 8
N_DEN, N_PROJ, N_T2, N_H, N_Y = 4, 2, 2, 24, 7
N_XHI, N_X1LO = 4, 4
N_COMB = 7 * EXPERTS
K_ST_USED = (0, 0, 1, 3, 3, 4)
QSCALE = HD ** -0.5

SETUP = (("wqk", 6 * 128), ("wv", C), ("wg", EXPERTS), ("w1", CHUNKS * 128), ("b2", EXPERTS * C),
         ("rel", HEADS * WW), ("lr", HEADS * WW), ("ul", HEADS * WW), ("sel", SPAN), ("selB", SPAN),
         ("vones", 2))
N_CONST = 6


def build(nc, x, packed, w2, wp, consts, out):
    ctx = ExitStack()
    with ctx:
        def sb(name, shape, dt=F32):
            return ctx.enter_context(nc.sbuf_tensor(name, shape, dt))

        def sem(name):
            return ctx.enter_context(nc.semaphore(name))

        bank = [None] * 8
        ps_s = ctx.enter_context(nc.psum_tensor("ps_s", [128, 1024], F32))
        ps_t = ctx.enter_context(nc.psum_tensor("ps_t", [128, 1024], F32))
        ps_o = ctx.enter_context(nc.psum_tensor("ps_o", [128, 512], F32))
        ps_f = ctx.enter_context(nc.psum_tensor("ps_f", [128, 1536], F32))
        bank[0:2] = [ps_s[:, 0:512], ps_s[:, 512:1024]]
        bank[2:4] = [ps_t[:, 0:512], ps_t[:, 512:1024]]
        bank[4] = ps_o[:, :]
        bank[5:8] = [ps_f[:, k * 512:(k + 1) * 512] for k in range(3)]

        ident = sb("ident", [128, 128])
        cst = sb("cst", [128, 3 + 16])
        qk_col = [cst[:, 0:1], cst[:, 1:2]]
        minus_half = cst[:, 2:3]
        tie = cst[0:LANES, 3:19].rearrange("p (e f) -> p e f", f=EXPERTS)
        den_rows = sb("den_rows", [C, C])
        sel16 = sb("sel16", [128, SPAN], F16)
        selB16 = sb("selB16", [128, SPAN], F16)
        ul16 = sb("ul16", [128, HEADS * WW], F16)
        bias16 = sb("bias16", [128, 2, HEADS * WW], F16)
        wqk_hi = sb("wqk_hi", [128, 6 * 128], F16)
        wqk_lo = sb("wqk_lo", [128, 6 * 128], F16)
        wv_hi = sb("wv_hi", [128, C], F16)
        wv_lo = sb("wv_lo", [128, C], F16)
        wg_hi = sb("wg_hi", [128, EXPERTS], F16)
        wg_lo = sb("wg_lo", [128, EXPERTS], F16)
        w1_hi = sb("w1_hi", [128, CHUNKS * 128], F16)
        w1_lo = sb("w1_lo", [128, CHUNKS * 128], F16)
        w2_sb = sb("w2_sb", [128, CHUNKS, C])
        wp_sb = sb("wp_sb", [C, 2, C])
        b2_16 = sb("b2_16", [128, EXPERTS * C], F16)
        ones16 = sb("ones16", [128, LANES], F16)

        xa = sb("xa", [LANES, UPI, W * C])
        stat1 = sb("stat1", [LANES, W, 6])
        mark = sb("mark", [LANES, 1])
        mv1 = sb("mv1", [LANES, W, 2])
        ve1 = sb("ve1", [LANES, W])
        rstd1 = sb("rstd1", [LANES, W])
        xn1 = sb("xn1", [LANES, W, C])
        x1_hi = sb("x1_hi", [128, TOK], F16)
        x1_lo = sb("x1_lo", [128, TOK], F16)
        split = sb("split", [128, 2, STRIP], F16)
        q_st = sb("q_st", [128, GROUPS, TOK], F16)
        k_st = sb("k_st", [128, 2, STRIP], F16)
        k_bd = sb("k_bd", [128, 2 * GROUPS, GH, STRIP], F16)
        v_bd = sb("v_bd", [128, 16 * PAIRS, 32])
        s_max = sb("s_max", [SPAN, HEADS])
        s_sub = sb("s_sub", [SPAN, HEADS, NB])
        p_sb = sb("p_sb", [128, HEADS, NB])
        pt_sb = sb("pt_sb", [128, PAIRS, 2 * WW])
        o_sb = sb("o_sb", [C, 2, TOK])

        xr = sb("xr", [LANES, UPI, W * C])
        rden = sb("rden", [C, STRIP])
        on_sb = sb("on_sb", [C, 2, TOK])
        stat2 = sb("stat2", [LANES, W, 6])
        mv2 = sb("mv2", [LANES, W, 2])
        ve2 = sb("ve2", [LANES, W])
        rstd2 = sb("rstd2", [LANES, W])
        xn2 = sb("xn2", [LANES, W, C])
        x2_hi = sb("x2_hi", [128, TOK], F16)
        x2_lo = sb("x2_lo", [128, TOK], F16)
        gmax = sb("gmax", [LANES, W])
        gsub = sb("gsub", [LANES, W, EXPERTS])
        gexp = sb("gexp", [LANES, W, EXPERTS])
        ggt = sb("ggt", [LANES, W * EXPERTS, EXPERTS])
        geq = sb("geq", [LANES, W * EXPERTS, EXPERTS])
        rank = sb("rank", [LANES, W * EXPERTS])
        gsel = sb("gsel", [LANES, W, EXPERTS])
        gtot = sb("gtot", [LANES, W])
        gden = sb("gden", [LANES, W])
        gate = sb("gate", [LANES, W * EXPERTS])
        g_sb = sb("g_sb", [128, CHUNKS, TOK])

        s_const = sem("s_const")
        s_zero = sem("s_zero")
        s_fill = sem("s_fill")
        s_ready = sem("s_ready")
        xa_in = [sem(f"xa_in{u}") for u in range(UPI)]
        xr_in = [sem(f"xr_in{u}") for u in range(UPI)]
        stored = [sem(f"stored{u}") for u in range(UPI)]
        t1_done, qk_done, v_done = sem("t1_done"), sem("qk_done"), sem("v_done")
        s_done, pt_done, o_done = sem("s_done"), sem("pt_done"), sem("o_done")
        den_done, proj_done, t2_done = sem("den_done"), sem("proj_done"), sem("t2_done")
        gate_done, h_done, y_done = sem("gate_done"), sem("h_done"), sem("y_done")
        x1hi_done, split_done, exp_done = sem("x1hi_done"), sem("split_done"), sem("exp_done")
        vodd_done, pta_done, o_saved = sem("vodd_done"), sem("pta_done"), sem("o_saved")
        x2hi_done, gexp_done, gelu_done = sem("x2hi_done"), sem("gexp_done"), sem("gelu_done")
        stat1_done, aggr1_done, var1_done = sem("stat1_done"), sem("aggr1_done"), sem("var1_done")
        rstd1_done, centre1_done, norm1_done = sem("rstd1_done"), sem("centre1_done"), sem("norm1_done")
        x1lo_done, stack_done, kbd_done = sem("x1lo_done"), sem("stack_done"), sem("kbd_done")
        veven_done, max_done, sub_done = sem("veven_done"), sem("max_done"), sem("sub_done")
        ptb_done = sem("ptb_done")
        rden_done, on_done, res_done = sem("rden_done"), sem("on_done"), sem("res_done")
        stat2_done, aggr2_done, var2_done = sem("stat2_done"), sem("aggr2_done"), sem("var2_done")
        rstd2_done, norm2_done, x2lo_done = sem("rstd2_done"), sem("norm2_done"), sem("x2lo_done")
        gate_ready = sem("gate_ready")
        router = sem("router")
        comb_done = sem("comb_done")

        N_ROUTER = 12
        tile_cols = LANES

        def windows(t):
            return t.rearrange("p (h w c r) -> p h w c r", h=2, w=NW, c=W)

        block = ctx.enter_context(nc.Block())

        LOOPS = B - 1

        def schedule(eng, step, prologue):
            prologue()
            with eng.Fori(0, LOOPS) as m:
                for u in range(UPI):
                    with eng.register(f"image_{u}") as counter:
                        eng.reg_mov(counter, m)
                        image = eng.snap(counter)
                        step((image, u), (image, u + 1), u)
            for u in range(UPI):
                step((LOOPS, u), (LOOPS, u + 1) if u < UPI - 1 else None, u)

        @block.sync
        def _(sp):
            def visit(unit, u):
                return (unit[0], (unit[1] - u) // UPI)

            def slot_at(unit, u, per, k):
                m, extra = visit(unit, u)
                return m * per + (extra * per + k)

            def load_a(unit, u, first=False):
                if not first:
                    sp.wait_ge(norm1_done, at((unit[0], unit[1] - UPI), 1, 1))
                img = unit[0] + unit[1] // UPI
                for lane, rows, row, cell, cols, col in piece_list(u, SHIFT_IN):
                    sp.dma_start(xa[lane:lane + rows, u, cell * C:(cell + cols) * C],
                                 x[img, row:row + rows, col * C:(col + cols) * C]
                                 ).then_inc(xa_in[u], 16)

            def load_r(unit, u, first=False):
                if not first:
                    n = 16 * len(piece_list(u, SHIFT_OUT))
                    sp.wait_ge(stored[u], slot_at((unit[0], unit[1] - UPI), u, n, n))
                img = unit[0] + unit[1] // UPI
                for lane, rows, row, cell, cols, col in piece_list(u, SHIFT_OUT):
                    sp.dma_start(xr[lane:lane + rows, u, cell * C:(cell + cols) * C],
                                 x[img, row:row + rows, col * C:(col + cols) * C]
                                 ).then_inc(xr_in[u], 16)

            def store(unit, u):
                sp.wait_ge(comb_done, at(unit, N_COMB, N_COMB))
                for lane, rows, row, cell, cols, col in piece_list(u, SHIFT_OUT):
                    sp.dma_start(out[unit[0], row:row + rows, col * C:(col + cols) * C],
                                 xr[lane:lane + rows, u, cell * C:(cell + cols) * C]
                                 ).then_inc(stored[u], 16)

            def prologue():
                for dst, src in ((g_sb[:, :, :].rearrange("p a b -> p (a b)")[:, 0:packed.shape[1]], packed),
                                 (ident[:, :], consts[:, 0:128]), (cst[:, :], consts[:, 128:147]),
                                 (den_rows[:, :], consts[0:C, 147:147 + C]), (w2_sb[:, :, :], w2),
                                 (wp_sb[:, :, :], wp)):
                    sp.dma_start(dst, src).then_inc(s_const, 16)
                for u in range(UPI):
                    load_a((0, u), u, first=True)
                for u in range(UPI):
                    load_r((0, u), u, first=True)

            def step(f, a, u):
                last_image = isinstance(f[0], int) and f[0] == B - 1
                if not last_image:
                    load_a((f[0], f[1] + UPI), u)
                store(f, u)
                if not last_image:
                    load_r((f[0], f[1] + UPI), u)

            schedule(sp, step, prologue)
            for u in range(UPI):
                sp.wait_ge(stored[u], 16 * len(piece_list(u, SHIFT_OUT)) * B)

        @block.gpsimd
        def _(pool):
            nc.gpsimd.memset(k_bd[:, :, :, :], 0.0).then_inc(s_zero, 1)
            nc.gpsimd.memset(v_bd[:, :, :], 0.0).then_inc(s_zero, 1)
            nc.gpsimd.memset(p_sb[:, :, :], 0.0).then_inc(s_zero, 1)

            def norm1(a):
                u = a[1] % UPI
                pool.wait_ge(var1_done, at(a, 1, 1))
                nc.gpsimd.tensor_tensor(rstd1[:, :], ve1[:, :], minus_half[0:LANES, :].broadcast_to([LANES, W]),
                                        ALU.pow).then_inc(rstd1_done, 1)
                if not first(a):
                    pool.wait_ge(t1_done, at(a, N_T1))
                wide = [LANES, W, C]
                nc.gpsimd.tensor_tensor(xn1[:, :, :], xa[:, u, :].rearrange("p (t c) -> p t c", c=C),
                                        mv1[:, :, 0:1].broadcast_to(wide), ALU.subtract
                                        ).then_inc(centre1_done, 1)
                pool.wait_ge(rstd1_done, at(a, 1, 1))
                pool.wait_ge(centre1_done, at(a, 1, 1))
                nc.gpsimd.tensor_tensor(xn1[:, :, :], xn1[:, :, :], rstd1[:, :].unsqueeze(2).broadcast_to(wide),
                                        ALU.mult).then_inc(norm1_done, 1)

            def rsqrt2(f):
                pool.wait_ge(var2_done, at(f, 1, 1))
                nc.gpsimd.tensor_tensor(rstd2[:, :], ve2[:, :], minus_half[0:LANES, :].broadcast_to([LANES, W]),
                                        ALU.pow).then_inc(rstd2_done, 1)

            def prologue():
                pool.wait_ge(s_ready, 1)
                norm1((0, 0))
                norm1((0, 1))

            def step(f, a, u):
                rsqrt2(f)
                if a is not None and not last(a):
                    norm1((a[0], a[1] + 1))

            schedule(pool, step, prologue)

        @block.scalar
        def _(act):
            def x1_high(a):
                for k, (j0, n) in enumerate(((0, 4), (4, 3))):
                    act.wait_ge(t1_done, at(a, N_T1, k + 1))
                    src = bank[2 + k][0:C, 0:n * LANES].rearrange("p (j h w r) -> p h j w r", h=2, w=NW, r=W)
                    dst = windows(x1_hi[0:C, :])
                    for half in range(2):
                        nc.scalar.activation(dst[:, half, :, j0:j0 + n, :].rearrange("p w j r -> p j w r"),
                                             src[:, half], ACT.Copy).then_inc(x1hi_done, 1)

            def v_odd(a):
                for k in range(2):
                    act.wait_ge(v_done, at(a, N_V, k + 1))
                    nc.scalar.activation(
                        v_bd[NB:SPAN, k * 48:(k + 1) * 48, HD:2 * HD],
                        bank[3 + k][NB:SPAN, 0:384].rearrange("p (n d) -> p n d", d=HD),
                        ACT.Copy, scale=1.0 / WSCALE).then_inc(vodd_done, 1)

            def qk_split(a, t):
                kind = (t // GROUPS) % 2
                act.wait_ge(qk_done, at(a, N_QK, t + 1))
                if t >= 2:
                    act.wait_ge(stack_done, at(a, N_QK, t - 1))
                elif not first(a):
                    act.wait_ge(stack_done, at(a, N_QK))
                nc.scalar.activation(split[:, t % 2, :], bank[t % 2][:, 0:STRIP], ACT.Copy,
                                     scale=qk_col[kind]).then_inc(split_done, 1)

            def x2_high(f):
                for k, (j0, n) in enumerate(((0, 4), (4, 3))):
                    act.wait_ge(t2_done, at(f, N_T2, k + 1))
                    nc.scalar.activation(x2_hi[0:C, j0 * LANES:(j0 + n) * LANES],
                                         bank[5 + k][0:C, 0:n * LANES], ACT.Copy).then_inc(x2hi_done, 1)

            def gate_exp(f):
                act.wait_ge(router, at(f, N_ROUTER, 2))
                nc.scalar.activation(gexp[:, :, :], gsub[:, :, :], ACT.Exp,
                                     scale=1.0 / WSCALE).then_inc(gexp_done, 1)

            def gelus(f):
                for k in range(N_H):
                    chunk, half = k // 2, k % 2
                    act.wait_ge(h_done, at(f, N_H, k + 1))
                    nc.scalar.activation(g_sb[:, chunk, half * STRIP:(half + 1) * STRIP],
                                         bank[5 + k % 2][:, 0:STRIP], ACT.Gelu,
                                         scale=1.0 / WSCALE).then_inc(gelu_done, 1)

            def exps(a, n):
                act.wait_ge(sub_done, at(a, N_S, n + 1))
                nc.scalar.activation(p_sb[0:SPAN, :, 0:WW], s_sub[:, :, 0:WW], ACT.Exp).then_inc(exp_done, 1)

            def copy_pt(a, n):
                act.wait_ge(pt_done, at(a, N_PT, 2 * n + 1))
                nc.scalar.activation(
                    pt_sb[0:SPAN, 0:4, :].rearrange("p h (s q) -> p h s q", s=2),
                    bank[2][0:SPAN, :].rearrange("p (h s q) -> p h s q", h=4, s=2)[:, :, :, 0:WW],
                    ACT.Copy).then_inc(pta_done, 1)

            def save_o(a, n):
                half, wr = n // 4, 2 * (n % 4)
                act.wait_ge(o_done, at(a, N_O, n + 1))
                dst = o_sb[:, :, :].rearrange("p b (c h r) -> p b c h r", c=W, h=2)
                nc.scalar.activation(dst[:, :, :, half, W * wr:W * (wr + 2)],
                                     ps_o[0:C, 0:4 * WW].rearrange("p (b c r) -> p b c r", b=2, c=W),
                                     ACT.Copy).then_inc(o_saved, 1)

            def pairs(a):
                for n in range(8):
                    exps(a, n)
                    copy_pt(a, n)
                    save_o(a, n)

            def prologue():
                act.wait_ge(s_ready, 1)
                x1_high((0, 0))
                v_odd((0, 0))
                for t in range(12):
                    qk_split((0, 0), t)
                pairs((0, 0))

            def step(f, a, u):
                if a is not None:
                    x1_high(a)
                    v_odd(a)
                    for t in range(4):
                        qk_split(a, t)
                x2_high(f)
                if a is not None:
                    for t in range(4, 12):
                        qk_split(a, t)
                gate_exp(f)
                gelus(f)
                if a is not None:
                    pairs(a)

            schedule(act, step, prologue)

        @block.vector
        def _(dve):
            fills = [0]

            def fill(ins):
                fills[0] += 1
                ins.then_inc(s_fill, 1)
                dve.wait_ge(s_fill, fills[0])

            V = nc.vector

            def setup():
                raw = g_sb[:, :, :].rearrange("p a b -> p (a b)")
                offs, o = {}, 0
                for name, n in SETUP:
                    offs[name] = raw[:, o:o + n]
                    o += n
                dve.wait_ge(s_const, 16 * N_CONST)
                dve.wait_ge(s_zero, 3)
                fill(V.tensor_copy(sel16[:, :], offs["sel"]))
                fill(V.tensor_copy(selB16[:, :], offs["selB"]))
                fill(V.tensor_copy(ul16[:, :], offs["ul"]))
                for src, hi, lo in (("wqk", wqk_hi, wqk_lo), ("wv", wv_hi, wv_lo),
                                    ("wg", wg_hi, wg_lo), ("w1", w1_hi, w1_lo)):
                    fill(V.tensor_scalar(hi[:, :], offs[src], WSCALE, None, ALU.mult))
                    fill(V.scalar_tensor_tensor(out=lo[:, :], in0=offs[src], scalar=WSCALE, in1=hi[:, :],
                                                op0=ALU.mult, op1=ALU.subtract))
                tmp = x1_hi[:, 0:384]
                fill(V.tensor_copy(tmp, offs["b2"]))
                fill(V.memset(b2_16[:, :], 0.0))
                fill(V.tensor_copy(b2_16[0:1, :], tmp[0:1, :]))
                fill(V.tensor_tensor(b2_16[32:33, :], offs["b2"][32:33, :], tmp[32:33, :], ALU.subtract))
                fill(V.memset(ones16[:, :], 1.0))
                tmp = x1_hi[:, 0:HEADS * WW]
                fill(V.tensor_copy(tmp, offs["rel"]))
                for v in range(2):
                    fill(V.tensor_tensor(bias16[NB:128, v, :], offs["rel"][NB:128, :], tmp[NB:128, :],
                                         ALU.subtract))
                fill(V.tensor_copy(bias16[0:NB, 0, :], tmp[0:NB, :]))
                fill(V.tensor_tensor(bias16[0:NB, 1, :], offs["rel"][0:NB, :], offs["lr"][0:NB, :], ALU.add))
                fill(V.tensor_copy(v_bd[:, :, 2 * HD:2 * HD + 2],
                                   offs["vones"].unsqueeze(1).broadcast_to([128, 16 * PAIRS, 2])))
                for hi, lo in ((x1_hi, x1_lo), (x2_hi, x2_lo)):
                    fill(V.memset(hi[ONES_ROW:128, :], 0.0))
                    fill(V.memset(hi[ONES_ROW:ONES_ROW + 1, :], 1.0))
                    fill(V.memset(lo[ONES_ROW:128, :], 0.0))
                V.memset(s_sub[:, :, :], 0.0).then_inc(s_ready, 1)
                dve.wait_ge(s_ready, 1)

            def ln1_stats(a):
                u = a[1] % UPI
                per = 16 * len(piece_list(u, SHIFT_IN))
                dve.wait_ge(xa_in[u], a[0] * per + (a[1] // UPI + 1) * per)
                if not first(a):
                    dve.wait_ge(norm1_done, at(a, 1))
                for t in range(W):
                    V.bn_stats(stat1[:, t, :], xa[:, u, t * C:(t + 1) * C]).then_inc(stat1_done, 1)
                dve.wait_ge(stat1_done, at(a, W, W))
                V.memset(mark[:, :], 0.0)
                for t in range(W):
                    V.bn_aggr(mv1[:, t, :], stat1[:, t, :]).then_inc(aggr1_done, 1)
                dve.wait_ge(aggr1_done, at(a, W, W))
                V.tensor_scalar(ve1[:, :], mv1[:, :, 1], EPS_C, None, ALU.add).then_inc(var1_done, 1)

            def x1_low(a):
                dst, hi = windows(x1_lo[0:C, :]), windows(x1_hi[0:C, :])
                for k, (j0, n) in enumerate(((0, 4), (4, 3))):
                    src = bank[2 + k][0:C, 0:n * LANES].rearrange("p (j h w r) -> p h j w r", h=2, w=NW, r=W)
                    for half in range(2):
                        dve.wait_ge(x1hi_done, at(a, N_XHI, 2 * k + 2))
                        V.tensor_tensor(dst[:, half, :, j0:j0 + n, :].rearrange("p w j r -> p j w r"),
                                        src[:, half],
                                        hi[:, half, :, j0:j0 + n, :].rearrange("p w j r -> p j w r"),
                                        ALU.subtract).then_inc(x1lo_done, 1)

            def v_even(a):
                for k in range(2):
                    dve.wait_ge(v_done, at(a, N_V, k + 1))
                    V.tensor_scalar(v_bd[0:WW, k * 48:(k + 1) * 48, 0:HD],
                                    bank[3 + k][0:WW, 0:384].rearrange("p (n d) -> p n d", d=HD),
                                    1.0 / WSCALE, None, ALU.mult).then_inc(veven_done, 1)

            def qk_stack(a, t):
                half, kind, g = t // 6, (t // GROUPS) % 2, t % GROUPS
                scale = (QSCALE if kind == 0 else 1.0) / WSCALE
                dst = q_st[:, g, half * STRIP:(half + 1) * STRIP] if kind == 0 else k_st[:, t % 2, :]
                if kind:
                    before = K_ST_USED[half * GROUPS + g]
                    if before or not first(a):
                        dve.wait_ge(kbd_done, at(a, 6 * GH, before * GH))
                dve.wait_ge(split_done, at(a, N_QK, t + 1))
                V.scalar_tensor_tensor(out=dst, in0=bank[t % 2][:, 0:STRIP], scalar=scale,
                                       in1=split[:, t % 2, :], op0=ALU.mult, op1=ALU.subtract
                                       ).then_inc(stack_done, 1)
                if kind:
                    dve.wait_ge(stack_done, at(a, N_QK, t + 1))
                    for j in range(GH):
                        rows = slice(32 * j, 32 * j + 32)
                        V.tensor_copy(k_bd[rows, half * GROUPS + g, j, :], k_st[rows, t % 2, :]
                                      ).then_inc(kbd_done, 1)

            def softmax_pair(a, n):
                scores = ps_s[0:SPAN, 0:HEADS * NB].rearrange("p (h k) -> p h k", k=NB)[:, :, 0:WW]
                dve.wait_ge(s_done, at(a, N_S, n + 1))
                V.tensor_reduce(s_max[:, :], scores, AX.X, ALU.max).then_inc(max_done, 1)
                dve.wait_ge(max_done, at(a, N_S, n + 1))
                V.tensor_tensor(s_sub[:, :, 0:WW], scores,
                                s_max[:, :].unsqueeze(2).broadcast_to([SPAN, HEADS, WW]),
                                ALU.subtract).then_inc(sub_done, 1)

            def copy_pt(a, n):
                dve.wait_ge(pt_done, at(a, N_PT, 2 * n + 2))
                V.tensor_copy(pt_sb[0:SPAN, 4:6, :].rearrange("p h (s q) -> p h s q", s=2),
                              bank[3][0:SPAN, 0:256].rearrange("p (h s q) -> p h s q", h=2, s=2)[:, :, :, 0:WW]
                              ).then_inc(ptb_done, 1)

            def normalise_o(f):
                for k in range(N_DEN):
                    half, blk = k // 2, k % 2
                    cols = slice(half * STRIP, (half + 1) * STRIP)
                    if k:
                        dve.wait_ge(on_done, at(f, N_DEN, k))
                    dve.wait_ge(den_done, at(f, N_DEN, k + 1))
                    V.reciprocal(rden[:, :], bank[5 + k % 3][0:C, 0:STRIP]).then_inc(rden_done, 1)
                    dve.wait_ge(rden_done, at(f, N_DEN, k + 1))
                    V.tensor_tensor(on_sb[:, blk, cols], o_sb[:, blk, cols], rden[:, :], ALU.mult
                                    ).then_inc(on_done, 1)

            def residual(f, u):
                per = 16 * len(piece_list(u, SHIFT_OUT))
                dve.wait_ge(xr_in[u], f[0] * per + per)
                for k, (j0, n) in enumerate(((0, 4), (4, 3))):
                    dve.wait_ge(proj_done, at(f, N_PROJ, k + 1))
                    slot = xr[:, u, j0 * C:(j0 + n) * C]
                    V.tensor_tensor(slot, bank[6 + k][0:LANES, 0:n * C], slot, ALU.add).then_inc(res_done, 1)

            def ln2_stats(f, u):
                for t in range(W):
                    dve.wait_ge(res_done, at(f, 2, 1 + t // 4))
                    V.bn_stats(stat2[:, t, :], xr[:, u, t * C:(t + 1) * C]).then_inc(stat2_done, 1)
                dve.wait_ge(stat2_done, at(f, W, W))
                V.memset(mark[:, :], 0.0)
                for t in range(W):
                    V.bn_aggr(mv2[:, t, :], stat2[:, t, :]).then_inc(aggr2_done, 1)
                dve.wait_ge(aggr2_done, at(f, W, W))
                V.tensor_scalar(ve2[:, :], mv2[:, :, 1], EPS_T, None, ALU.add).then_inc(var2_done, 1)

            def ln2_norm(f, u):
                dve.wait_ge(rstd2_done, at(f, 1, 1))
                for t in range(W):
                    V.tensor_scalar(xn2[:, t, :], xr[:, u, t * C:(t + 1) * C], mv2[:, t, 0:1],
                                    rstd2[:, t:t + 1], ALU.subtract, ALU.mult).then_inc(norm2_done, 1)

            def x2_low(f):
                for k, (j0, n) in enumerate(((0, 4), (4, 3))):
                    cols = slice(j0 * LANES, (j0 + n) * LANES)
                    dve.wait_ge(x2hi_done, at(f, 2, k + 1))
                    V.tensor_tensor(x2_lo[0:C, cols], bank[5 + k][0:C, 0:n * LANES], x2_hi[0:C, cols],
                                    ALU.subtract).then_inc(x2lo_done, 1)

            def router_a(f):
                sc = bank[7][0:LANES, 0:W * EXPERTS].rearrange("p (t e) -> p t e", e=EXPERTS)
                dve.wait_ge(gate_done, at(f, 1, 1))
                V.tensor_reduce(gmax[:, :], sc, AX.X, ALU.max).then_inc(router, 1)
                dve.wait_ge(router, at(f, N_ROUTER, 1))
                V.tensor_tensor(gsub[:, :, :], sc, gmax[:, :].unsqueeze(2).broadcast_to([LANES, W, EXPERTS]),
                                ALU.subtract).then_inc(router, 1)

            def router_b(f):
                k = [2]

                def link(ins):
                    k[0] += 1
                    ins.then_inc(router, 1)
                    dve.wait_ge(router, at(f, N_ROUTER, k[0]))

                ge = gexp[:, :, :]
                mine = ge.rearrange("p t e -> p (t e)").unsqueeze(2).broadcast_to([LANES, W * EXPERTS, EXPERTS])
                mine = mine.rearrange("p (t e) f -> p t e f", e=EXPERTS)
                other = ge.unsqueeze(2).broadcast_to([LANES, W, EXPERTS, EXPERTS])
                gt4 = ggt[:, :, :].rearrange("p (t e) f -> p t e f", e=EXPERTS)
                eq4 = geq[:, :, :].rearrange("p (t e) f -> p t e f", e=EXPERTS)
                dve.wait_ge(gexp_done, at(f, 1, 1))
                V.tensor_tensor(gt4, other, mine, ALU.is_gt).then_inc(router, 1)
                k[0] += 1
                link(V.tensor_tensor(eq4, other, mine, ALU.is_equal))
                link(V.tensor_tensor(eq4, eq4, tie.unsqueeze(1).broadcast_to([LANES, W, EXPERTS, EXPERTS]),
                                     ALU.mult))
                link(V.tensor_tensor(ggt[:, :, :], ggt[:, :, :], geq[:, :, :], ALU.add))
                link(V.tensor_reduce(rank[:, :], ggt[:, :, :], AX.X, ALU.add))
                link(V.scalar_tensor_tensor(out=gsel[:, :, :].rearrange("p t e -> p (t e)"), in0=rank[:, :],
                                            scalar=1.5, in1=ge.rearrange("p t e -> p (t e)"),
                                            op0=ALU.is_lt, op1=ALU.mult))
                V.tensor_reduce(gtot[:, :], ge, AX.X, ALU.add).then_inc(router, 1)
                k[0] += 1
                link(V.tensor_reduce(gden[:, :], gsel[:, :, :], AX.X, ALU.add))
                link(V.scalar_tensor_tensor(out=gden[:, :], in0=gtot[:, :], scalar=1e-9, in1=gden[:, :],
                                            op0=ALU.mult, op1=ALU.add))
                link(V.reciprocal(gden[:, :], gden[:, :]))
                assert k[0] == N_ROUTER
                V.tensor_tensor(gate[:, :].rearrange("p (t e) -> p t e", e=EXPERTS), gsel[:, :, :],
                                gden[:, :].unsqueeze(2).broadcast_to([LANES, W, EXPERTS]),
                                ALU.mult).then_inc(gate_ready, 1)
                dve.wait_ge(gate_ready, at(f, 1, 1))

            def combine(f, u, j):
                slot = xr[:, u, j * C:(j + 1) * C]
                dve.wait_ge(y_done, at(f, N_Y, j + 1))
                for e in range(EXPERTS):
                    V.scalar_tensor_tensor(out=slot, in0=bank[7][0:LANES, e * C:(e + 1) * C],
                                           scalar=gate[:, j * EXPERTS + e:j * EXPERTS + e + 1], in1=slot,
                                           op0=ALU.mult, op1=ALU.add).then_inc(comb_done, 1)
                    dve.wait_ge(comb_done, at(f, N_COMB, j * EXPERTS + e + 1))

            def prologue():
                setup()
                ln1_stats((0, 0))
                x1_low((0, 0))
                ln1_stats((0, 1))
                v_even((0, 0))
                for t in range(12):
                    qk_stack((0, 0), t)
                for n in range(8):
                    softmax_pair((0, 0), n)
                    copy_pt((0, 0), n)

            def step(f, a, u):
                normalise_o(f)
                if a is not None:
                    x1_low(a)
                residual(f, u)
                ln2_stats(f, u)
                if a is not None:
                    v_even(a)
                    for t in range(2):
                        qk_stack(a, t)
                ln2_norm(f, u)
                if a is not None:
                    for t in range(2, 4):
                        qk_stack(a, t)
                x2_low(f)
                if a is not None:
                    for t in range(4, 12):
                        qk_stack(a, t)
                router_a(f)
                if a is not None and not last(a):
                    ln1_stats((a[0], a[1] + 1))
                router_b(f)
                for n in range(8):
                    if a is not None:
                        if n == 0:
                            softmax_pair(a, 0)
                        copy_pt(a, n)
                        if n < 7:
                            softmax_pair(a, n + 1)
                    if n < 7:
                        combine(f, u, n)

            schedule(dve, step, prologue)

        @block.tensor
        def _(pe):
            T = nc.tensor

            def three(outp, lhs_hi, lhs_lo, rhs_hi, rhs_lo, start=True):
                T.matmul(outp, lhs_hi, rhs_hi, start=start, stop=False, skip_group_check=True)
                T.matmul(outp, lhs_hi, rhs_lo, start=False, stop=False, skip_group_check=True)
                return T.matmul(outp, lhs_lo, rhs_hi, start=False, stop=True, skip_group_check=True)

            def transpose1(a):
                pe.wait_ge(norm1_done, at(a, 1, 1))
                for k, (j0, n) in enumerate(((0, 4), (4, 3))):
                    for j in range(n):
                        ins = T.transpose(bank[2 + k][0:C, j * LANES:(j + 1) * LANES], xn1[:, j0 + j, :],
                                          ident[0:LANES, 0:LANES])
                    ins.then_inc(t1_done, 1)

            def values(a):
                pe.wait_ge(x1lo_done, at(a, N_X1LO, N_X1LO))
                if not first(a):
                    pe.wait_ge(o_saved, at(a, N_O))
                for k in range(2):
                    for w in range(8):
                        x0 = (k * 8 + w) * WW
                        xh, xl = x1_hi[:, x0:x0 + WW], x1_lo[:, x0:x0 + WW]
                        for odd in range(2):
                            o = bank[3 + k][NB * odd:NB * odd + WW, w * 48:(w + 1) * 48]
                            wcols = slice(48 * odd, 48 * odd + 48)
                            ins = three(o, xh, xl, wv_hi[:, wcols], wv_lo[:, wcols])
                    ins.then_inc(v_done, 1)

            def qk(a, t):
                half, col = t // 6, (t % 6) * 128
                if t >= 2:
                    pe.wait_ge(stack_done, at(a, N_QK, t - 1))
                elif not first(a):
                    pe.wait_ge(sub_done, at(a, N_S))
                cols = slice(half * STRIP, (half + 1) * STRIP)
                three_w(bank[t % 2][:, 0:STRIP], wqk_hi[:, col:col + 128], wqk_lo[:, col:col + 128],
                        x1_hi[:, cols], x1_lo[:, cols]).then_inc(qk_done, 1)

            def three_w(outp, w_hi, w_lo, x_hi, x_lo):
                return three(outp, w_hi, w_lo, x_hi, x_lo)

            def scores(a, n):
                half, wr = n // 4, 2 * (n % 4)
                if n == 0:
                    pe.wait_ge(stack_done, at(a, N_QK, N_QK))
                    pe.wait_ge(kbd_done, at(a, 6 * GH, 6 * GH))
                else:
                    pe.wait_ge(sub_done, at(a, N_S, n))
                variant = 1 if half == 1 and a[1] % UPI == UPI - 1 else 0
                s3 = ps_s[0:SPAN, 0:HEADS * NB].rearrange("p (h k) -> p h k", k=NB)
                for h0, h1 in ((0, 8), (8, 12)):
                    T.matmul(s3[:, h0:h1, 0:WW], sel16[:, :], bias16[:, variant, h0 * WW:h1 * WW],
                             start=True, stop=False, skip_group_check=True)
                    if wr == NW - 2:
                        T.matmul(s3[:, h0:h1, 0:WW], selB16[:, :], ul16[:, h0 * WW:h1 * WW],
                                 start=False, stop=False, skip_group_check=True)
                for s in range(2):
                    x0 = half * STRIP + (wr + s) * WW
                    k0 = (wr + s) * WW
                    part = ps_s[NB * s:NB * s + WW, 0:HEADS * NB].rearrange("p (h k) -> p h k", k=NB)
                    for g in range(GROUPS):
                        ins = T.matmul(part[:, g * GH:(g + 1) * GH, 0:WW], q_st[:, g, x0:x0 + WW],
                                       k_bd[:, half * GROUPS + g, :, k0:k0 + WW],
                                       start=False, stop=True, skip_group_check=True)
                ins.then_inc(s_done, 1)

            def transpose_p(a, n):
                if n == 0:
                    pe.wait_ge(vodd_done, at(a, 2, 2))
                    pe.wait_ge(veven_done, at(a, 2, 2))
                pe.wait_ge(exp_done, at(a, N_S, n + 1))
                for p in range(PAIRS):
                    ins = T.transpose(bank[2 + p // 4][0:SPAN, (p % 4) * 128:(p % 4) * 128 + SPAN],
                                      p_sb[0:SPAN, 2 * p:2 * p + 2, :].rearrange("p h k -> p (h k)")[:, 0:SPAN],
                                      ident[0:SPAN, 0:SPAN])
                    if p in (3, 5):
                        ins.then_inc(pt_done, 1)

            def attend(a, n):
                half, wr = n // 4, 2 * (n % 4)
                pe.wait_ge(pta_done, at(a, N_S, n + 1))
                pe.wait_ge(ptb_done, at(a, N_S, n + 1))
                if n:
                    pe.wait_ge(o_saved, at(a, N_O, n))
                for s in range(2):
                    win = half * NW + wr + s
                    for p in range(PAIRS):
                        rows = slice(32 * (p % 3), 32 * (p % 3) + 32)
                        o = ps_o[rows, (p // 3) * 98:(p // 3) * 98 + 98]
                        o = o.rearrange("p (c s r) -> p c s r", c=W, s=2)[:, :, s, :]
                        ins = T.matmul(o, v_bd[0:SPAN, win * PAIRS + p, :], pt_sb[0:SPAN, p, s * WW:(s + 1) * WW],
                                       start=True, stop=True, skip_group_check=True)
                ins.then_inc(o_done, 1)

            def denominators(f):
                pe.wait_ge(o_saved, at(f, N_O, N_O))
                for k in range(N_DEN):
                    half, blk = k // 2, k % 2
                    if k == 3:
                        pe.wait_ge(rden_done, at(f, N_DEN, 1))
                    T.matmul(bank[5 + k % 3][0:C, 0:STRIP], den_rows[:, :],
                             o_sb[:, blk, half * STRIP:(half + 1) * STRIP],
                             start=True, stop=True).then_inc(den_done, 1)

            def project(f):
                pe.wait_ge(on_done, at(f, N_DEN, N_DEN))
                for k, (j0, n) in enumerate(((0, 4), (4, 3))):
                    for j in range(n):
                        for blk in range(2):
                            ins = T.matmul(bank[6 + k][0:LANES, j * C:(j + 1) * C],
                                           on_sb[:, blk, (j0 + j) * LANES:(j0 + j + 1) * LANES],
                                           wp_sb[:, blk, :], start=(blk == 0), stop=(blk == 1))
                    ins.then_inc(proj_done, 1)

            def transpose2(f):
                pe.wait_ge(norm2_done, at(f, W, W))
                for k, (j0, n) in enumerate(((0, 4), (4, 3))):
                    for j in range(n):
                        ins = T.transpose(bank[5 + k][0:C, j * LANES:(j + 1) * LANES], xn2[:, j0 + j, :],
                                          ident[0:LANES, 0:LANES])
                    ins.then_inc(t2_done, 1)

            def gate_scores(f):
                pe.wait_ge(x2lo_done, at(f, 2, 2))
                for j in range(W):
                    cols = slice(j * LANES, (j + 1) * LANES)
                    ins = three(bank[7][0:LANES, j * EXPERTS:(j + 1) * EXPERTS], x2_hi[:, cols],
                                x2_lo[:, cols], wg_hi[:, :], wg_lo[:, :])
                ins.then_inc(gate_done, 1)

            def hidden(f):
                for k in range(N_H):
                    chunk, half = k // 2, k % 2
                    if k >= 2:
                        pe.wait_ge(gelu_done, at(f, N_H, k - 1))
                    wc = slice(chunk * 128, (chunk + 1) * 128)
                    xc = slice(half * STRIP, (half + 1) * STRIP)
                    three_w(bank[5 + k % 2][:, 0:STRIP], w1_hi[:, wc], w1_lo[:, wc],
                            x2_hi[:, xc], x2_lo[:, xc]).then_inc(h_done, 1)

            def experts(f, j):
                if j == 0:
                    pe.wait_ge(gelu_done, at(f, N_H, N_H))
                    pe.wait_ge(router, at(f, N_ROUTER, 2))
                else:
                    pe.wait_ge(comb_done, at(f, N_COMB, j * EXPERTS))
                T.matmul(bank[7][0:LANES, 0:EXPERTS * C], ones16[:, :], b2_16[:, :],
                         start=True, stop=False, skip_group_check=True)
                for e in range(EXPERTS):
                    for c in range(CPE):
                        ins = T.matmul(bank[7][0:LANES, e * C:(e + 1) * C],
                                       g_sb[:, e * CPE + c, j * LANES:(j + 1) * LANES],
                                       w2_sb[:, e * CPE + c, :], start=False, stop=(c == CPE - 1),
                                       skip_group_check=True)
                ins.then_inc(y_done, 1)

            def prologue():
                pe.wait_ge(s_ready, 1)
                transpose1((0, 0))
                values((0, 0))
                for t in range(12):
                    qk((0, 0), t)
                for n in range(8):
                    scores((0, 0), n)
                    transpose_p((0, 0), n)
                    attend((0, 0), n)

            def step(f, a, u):
                denominators(f)
                if a is not None:
                    transpose1(a)
                project(f)
                if a is not None:
                    values(a)
                    for t in range(4):
                        qk(a, t)
                transpose2(f)
                if a is not None:
                    for t in range(4, 12):
                        qk(a, t)
                gate_scores(f)
                hidden(f)
                if a is not None:
                    scores(a, 0)
                for n in range(8):
                    if n < 7:
                        experts(f, n)
                    if a is not None:
                        transpose_p(a, n)
                        if n < 7:
                            scores(a, n + 1)
                        attend(a, n)

            schedule(pe, step, prologue)


def _rows(a, rows=128):
    out = np.zeros((rows,) + a.shape[1:], a.dtype)
    out[:a.shape[0]] = a
    return out


def _layout(w_qkv, b_qkv, w_proj, b_proj, rel_table, gate_w, gate_b, w1, b1, w2, b2):
    f = np.float32
    wb = np.concatenate([w_qkv.T, b_qkv[None]], 0)
    qk = wb[:, :2 * C].reshape(97, 2, HEADS, 1, HD)
    wqk = np.zeros((97, 2, HEADS, 4, HD), f)
    wqk[:, :, :, 0:3] = qk
    wqk = wqk.reshape(97, 768)
    wv = wb[:, 2 * C:].reshape(97, PAIRS, 2, HD).transpose(0, 2, 1, 3).reshape(97, C)
    wg = np.concatenate([gate_w, gate_b[None]], 0)
    w1b = np.concatenate([w1.transpose(1, 0, 2).reshape(C, EXPERTS * HID), b1.reshape(1, -1)], 0)
    b2r = np.zeros((128, EXPERTS * C), f)
    b2r[0] = b2r[32] = b2.reshape(-1)
    col, row = np.arange(WW) // W, np.arange(WW) % W
    idx = (row[:, None] - row[None] + W - 1) * (2 * W - 1) + (col[:, None] - col[None] + W - 1)
    rel = np.zeros((128, HEADS, WW), f)
    rel[0:WW] = rel[NB:SPAN] = rel_table[idx].transpose(0, 2, 1)
    late = lambda v: v >= W - W // 2
    lr, ul = np.zeros((128, HEADS, WW), f), np.zeros((128, HEADS, WW), f)
    lr[0:WW] = np.where(late(col)[:, None] != late(col)[None], MASKED, 0.0)[:, None, :]
    ul[0:WW] = np.where(late(row)[:, None] != late(row)[None], MASKED, 0.0)[:, None, :]
    sel, selB = np.zeros((128, SPAN), f), np.zeros((128, SPAN), f)
    q = np.arange(WW)
    for k0 in (0, NB):
        for m0 in (0, NB):
            sel[k0 + q, m0 + q] = 1.0
    selB[q, NB + q] = 1.0
    vones = np.zeros((128, 2), f)
    vones[0:WW, 0] = vones[NB:SPAN, 1] = 1.0
    parts = {"wqk": _rows(wqk), "wv": _rows(wv), "wg": _rows(wg), "w1": _rows(w1b), "b2": b2r,
             "rel": rel.reshape(128, -1), "lr": lr.reshape(128, -1), "ul": ul.reshape(128, -1),
             "sel": sel, "selB": selB, "vones": vones}
    packed = np.concatenate([parts[name] for name, _ in SETUP], 1).astype(f)
    wp = np.zeros((2, 3, 32, C), f)
    wp[:, :, 0:16] = w_proj.T.reshape(2, 3, 16, C)
    wp[0, 0, 16] = b_proj
    wp = np.ascontiguousarray(wp.reshape(2, C, C).transpose(1, 0, 2))
    w2p = np.ascontiguousarray(w2.reshape(EXPERTS, CPE, 128, C).transpose(2, 0, 1, 3).reshape(128, CHUNKS, C))
    consts = np.zeros((128, 147 + C), f)
    consts[:, 0:128] = np.eye(128)
    rep = np.arange(128) % 32 // HD
    consts[:, 128] = np.where(rep == 2, QSCALE / WSCALE, 0.0)
    consts[:, 129] = np.where(rep == 1, 1.0 / WSCALE, 0.0)
    consts[:, 130] = -0.5
    e = np.arange(EXPERTS)
    consts[:, 131:147] = (e[None, :] < e[:, None]).astype(f).reshape(1, -1)
    m = np.arange(C)
    odd = ((m % 32 >= HD) & (m % 32 < 2 * HD)) | (m % 32 == 17)
    consts[m // 32 * 32 + np.where(odd, 17, 16), 147 + m] = 1.0
    return packed, w2p, wp, consts


def kernel(**inputs):
    import concourse.bacc as bacc
    from concourse.bass_utils import run_bass_kernel_spmd

    a = {k: np.asarray(v) for k, v in inputs.items()}
    c, g = "L0_conv_", "L0_ffn_"
    packed, w2, wp, consts = _layout(a[c + "w_qkv"], a[c + "b_qkv"], a[c + "w_proj"], a[c + "b_proj"],
                                     a[c + "rel_table"], a[g + "gate_w"], a[g + "gate_b"],
                                     a[g + "w1"], a[g + "b1"], a[g + "w2"], a[g + "b2"])
    arrays = {"x": np.ascontiguousarray(a["x"]).reshape(B, IMG, IMG * C), "packed": packed, "w2": w2,
              "wp": wp, "consts": consts}
    nc = bacc.Bacc("TRN2", target_bir_lowering=False, num_devices=1)
    aps = [nc.dram_tensor(n, v.shape, F32, kind="ExternalInput").ap() for n, v in arrays.items()]
    out = nc.dram_tensor("out", (B, IMG, IMG * C), F32, kind="ExternalOutput").ap()
    build(nc, *aps, out)
    r = run_bass_kernel_spmd(nc, [arrays], core_ids=[0])
    return r.results[0]["out"].reshape(B, IMG, IMG, C)
```

```python
from contextlib import ExitStack

import numpy as np

import concourse.bass as bass
from concourse import mybir

F32 = mybir.dt.float32
F16 = mybir.dt.float16
ALU = mybir.AluOpType
ACT = mybir.ActivationFunctionType
AX = mybir.AxisListType

B, IMG, C = 32, 56, 96
W = 7
WW = W * W
NW = IMG // W
HEADS, HD = 12, 8
PAIRS = HEADS // 2
GROUPS, GH = 3, 4
EXPERTS, HID = 4, 384
CHUNKS = EXPERTS * HID // 128
CPE = HID // 128
UPI = 4
UNITS = B * UPI
WPAD = 64
STRIP = W * IMG
TOK = 2 * STRIP
LANES = 2 * IMG
NB = 64
SPAN = NB + WW
SHIFT_IN, SHIFT_OUT = 4, 3
WSCALE = 64.0
EPS_C, EPS_T = 1e-6, 1e-5
ONES_ROW = 96
MASKED = -60000.0


def at(unit, per_unit, k=0):
    m, c = unit
    return m * (UPI * per_unit) + (c * per_unit + k)


def first(unit):
    return isinstance(unit[0], int) and unit == (0, 0)


def last(unit):
    return isinstance(unit[0], int) and unit == (B - 1, UPI - 1)


def piece_list(u, shift):
    out = []
    for half in range(2):
        c0 = (half * IMG // 2 + u * W + shift)
        runs = []
        n0 = min(W, max(0, IMG - c0))
        if n0:
            runs.append((0, n0, c0))
        if n0 < W:
            runs.append((n0, W - n0, (c0 + n0) % IMG))
        for r0, rows, row in ((0, IMG - shift, shift), (IMG - shift, shift, 0)):
            for cell, cols, col in runs:
                out.append((half * IMG + r0, rows, row, cell, cols, col))
    return out


N_T1, N_QK, N_V, N_S, N_PT, N_O = 2, 12, 2, 8, 16, 8
N_PROJ, N_T2, N_H, N_Y = 2, 2, 24, 7
N_XHI, N_X1LO = 4, 4
N_COMB = 7 * EXPERTS
K_ST_USED = (0, 0, 1, 3, 3, 4)
QSCALE = HD ** -0.5

N_XV = 4

SETUP = (("wqk", 6 * 128), ("wv", C), ("wg", EXPERTS), ("w1", CHUNKS * 128), ("b2", EXPERTS * C),
         ("rel", HEADS * WW), ("lr", HEADS * WW), ("ul", HEADS * WW), ("sel", SPAN), ("selB", SPAN))
N_CONST = 5


def build(nc, x, packed, w2, wp, consts, out):
    ctx = ExitStack()
    with ctx:
        def sb(name, shape, dt=F32):
            return ctx.enter_context(nc.sbuf_tensor(name, shape, dt))

        def sem(name):
            return ctx.enter_context(nc.semaphore(name))

        bank = [None] * 8
        ps_s = ctx.enter_context(nc.psum_tensor("ps_s", [128, 1024], F32))
        ps_t = ctx.enter_context(nc.psum_tensor("ps_t", [128, 1024], F32))
        ps_o = ctx.enter_context(nc.psum_tensor("ps_o", [128, 512], F32))
        ps_f = ctx.enter_context(nc.psum_tensor("ps_f", [128, 1536], F32))
        bank[0:2] = [ps_s[:, 0:512], ps_s[:, 512:1024]]
        bank[2:4] = [ps_t[:, 0:512], ps_t[:, 512:1024]]
        bank[4] = ps_o[:, :]
        bank[5:8] = [ps_f[:, k * 512:(k + 1) * 512] for k in range(3)]

        ident = sb("ident", [128, 128])
        cst = sb("cst", [128, 3 + 16])
        qk_col = [cst[:, 0:1], cst[:, 1:2]]
        minus_half = cst[:, 2:3]
        tie = cst[0:LANES, 3:19].rearrange("p (e f) -> p e f", f=EXPERTS)
        sel16 = sb("sel16", [128, SPAN], F16)
        selB16 = sb("selB16", [128, SPAN], F16)
        ul16 = sb("ul16", [128, HEADS * WW], F16)
        bias16 = sb("bias16", [128, 2, HEADS * WW], F16)
        wqk_hi = sb("wqk_hi", [128, 6 * 128], F16)
        wqk_lo = sb("wqk_lo", [128, 6 * 128], F16)
        wv_hi = sb("wv_hi", [128, C], F16)
        wv_lo = sb("wv_lo", [128, C], F16)
        wg_hi = sb("wg_hi", [128, EXPERTS], F16)
        wg_lo = sb("wg_lo", [128, EXPERTS], F16)
        w1_hi = sb("w1_hi", [128, CHUNKS * 128], F16)
        w1_lo = sb("w1_lo", [128, CHUNKS * 128], F16)
        w2_sb = sb("w2_sb", [128, CHUNKS, C])
        wp_sb = sb("wp_sb", [128, 2, C])
        b2_16 = sb("b2_16", [128, EXPERTS * C], F16)
        ones16 = sb("ones16", [128, LANES], F16)

        xa = sb("xa", [LANES, UPI, W * C])
        stat1 = sb("stat1", [LANES, W, 6])
        mark = sb("mark", [LANES, 1])
        mv1 = sb("mv1", [LANES, W, 2])
        ve1 = sb("ve1", [LANES, W])
        rstd1 = sb("rstd1", [LANES, W])
        xn1 = sb("xn1", [LANES, W, C])
        x1_hi = sb("x1_hi", [128, 16 * WPAD], F16)
        x1_lo = sb("x1_lo", [128, 16 * WPAD], F16)
        split = sb("split", [128, 2, STRIP], F16)
        q_st = sb("q_st", [128, GROUPS, TOK], F16)
        k_st = sb("k_st", [128, 2, STRIP], F16)
        k_bd = sb("k_bd", [128, 2 * GROUPS, GH, STRIP], F16)
        v_bd = sb("v_bd", [128, 16 * PAIRS, 32])
        s_max = sb("s_max", [SPAN, HEADS])
        s_sub = sb("s_sub", [SPAN, HEADS, NB])
        s_sum = sb("s_sum", [SPAN, HEADS])
        s_rec = sb("s_rec", [SPAN, HEADS])
        p_sb = sb("p_sb", [128, 2, HEADS, NB])
        pt_sb = sb("pt_sb", [128, PAIRS, 2 * WW])
        o_sb = sb("o_sb", [128, 2, TOK])

        xr = sb("xr", [LANES, UPI, W * C])
        stat2 = sb("stat2", [LANES, W, 6])
        mv2 = sb("mv2", [LANES, W, 2])
        ve2 = sb("ve2", [LANES, W])
        rstd2 = sb("rstd2", [LANES, W])
        xn2 = sb("xn2", [LANES, W, C])
        x2_hi = sb("x2_hi", [128, TOK], F16)
        x2_lo = sb("x2_lo", [128, TOK], F16)
        gmax = sb("gmax", [LANES, W])
        gsub = sb("gsub", [LANES, W, EXPERTS])
        gexp = sb("gexp", [LANES, W, EXPERTS])
        ggt = sb("ggt", [LANES, W * EXPERTS, EXPERTS])
        geq = sb("geq", [LANES, W * EXPERTS, EXPERTS])
        rank = sb("rank", [LANES, W * EXPERTS])
        gsel = sb("gsel", [LANES, W, EXPERTS])
        gtot = sb("gtot", [LANES, W])
        gden = sb("gden", [LANES, W])
        gate = sb("gate", [LANES, W * EXPERTS])
        g_sb = sb("g_sb", [128, CHUNKS, TOK])

        s_const = sem("s_const")
        s_zero = sem("s_zero")
        s_fill = sem("s_fill")
        s_ready = sem("s_ready")
        xa_in = [sem(f"xa_in{u}") for u in range(UPI)]
        xr_in = [sem(f"xr_in{u}") for u in range(UPI)]
        stored = [sem(f"stored{u}") for u in range(UPI)]
        t1_done, qk_done, v_done = sem("t1_done"), sem("qk_done"), sem("v_done")
        s_done, pt_done, o_done = sem("s_done"), sem("pt_done"), sem("o_done")
        proj_done, t2_done = sem("proj_done"), sem("t2_done")
        gate_done, h_done, y_done = sem("gate_done"), sem("h_done"), sem("y_done")
        x1hi_done, split_done, exp_done = sem("x1hi_done"), sem("split_done"), sem("exp_done")
        vact_done, pta_done, o_saved = sem("vact_done"), sem("pta_done"), sem("o_saved")
        x2hi_done, gexp_done, gelu_done = sem("x2hi_done"), sem("gexp_done"), sem("gelu_done")
        stat1_done, aggr1_done, var1_done = sem("stat1_done"), sem("aggr1_done"), sem("var1_done")
        rstd1_done, centre1_done, norm1_done = sem("rstd1_done"), sem("centre1_done"), sem("norm1_done")
        x1lo_done, stack_done, kbd_done = sem("x1lo_done"), sem("stack_done"), sem("kbd_done")
        vdve_done, max_done, sub_done = sem("vdve_done"), sem("max_done"), sem("sub_done")
        ptb_done = sem("ptb_done")
        sum_done, rec_done, pnorm_done = sem("sum_done"), sem("rec_done"), sem("pnorm_done")
        res_done = sem("res_done")
        stat2_done, aggr2_done, var2_done = sem("stat2_done"), sem("aggr2_done"), sem("var2_done")
        rstd2_done, norm2_done, x2lo_done = sem("rstd2_done"), sem("norm2_done"), sem("x2lo_done")
        gate_ready = sem("gate_ready")
        router = sem("router")
        comb_done = sem("comb_done")

        N_ROUTER = 12
        tile_cols = LANES

        def windows(t):
            t = t.rearrange("p (h w k) -> p h w k", h=2, k=WPAD)[:, :, :, 0:WW]
            return t.rearrange("p h w (c r) -> p h w c r", c=W)

        def v_src(k, s, odd):
            src = bank[3 + k][NB * s:NB * s + WW, 0:4 * C].rearrange("p (n z) -> p n z", z=C)
            return src[:, :, 48 * odd:48 * odd + 48].rearrange("p n (h d) -> p n h d", d=HD)

        def v_dst(k, s, odd):
            dst = v_bd[NB * odd:NB * odd + WW, k * 48:(k + 1) * 48, HD * odd:HD * (odd + 1)]
            return dst.rearrange("p (n s h) d -> p n s h d", s=2, h=PAIRS)[:, :, s]

        block = ctx.enter_context(nc.Block())

        LOOPS = B - 1

        def schedule(eng, step, prologue):
            prologue()
            with eng.Fori(0, LOOPS) as m:
                for u in range(UPI):
                    with eng.register(f"image_{u}") as counter:
                        eng.reg_mov(counter, m)
                        image = eng.snap(counter)
                        step((image, u), (image, u + 1), u)
            for u in range(UPI):
                step((LOOPS, u), (LOOPS, u + 1) if u < UPI - 1 else None, u)

        @block.sync
        def _(sp):
            def visit(unit, u):
                return (unit[0], (unit[1] - u) // UPI)

            def slot_at(unit, u, per, k):
                m, extra = visit(unit, u)
                return m * per + (extra * per + k)

            def load_a(unit, u, first=False):
                if not first:
                    sp.wait_ge(norm1_done, at((unit[0], unit[1] - UPI), 1, 1))
                img = unit[0] + unit[1] // UPI
                for lane, rows, row, cell, cols, col in piece_list(u, SHIFT_IN):
                    sp.dma_start(xa[lane:lane + rows, u, cell * C:(cell + cols) * C],
                                 x[img, row:row + rows, col * C:(col + cols) * C]
                                 ).then_inc(xa_in[u], 16)

            def load_r(unit, u, first=False):
                if not first:
                    n = 16 * len(piece_list(u, SHIFT_OUT))
                    sp.wait_ge(stored[u], slot_at((unit[0], unit[1] - UPI), u, n, n))
                img = unit[0] + unit[1] // UPI
                for lane, rows, row, cell, cols, col in piece_list(u, SHIFT_OUT):
                    sp.dma_start(xr[lane:lane + rows, u, cell * C:(cell + cols) * C],
                                 x[img, row:row + rows, col * C:(col + cols) * C]
                                 ).then_inc(xr_in[u], 16)

            def store(unit, u):
                sp.wait_ge(comb_done, at(unit, N_COMB, N_COMB))
                for lane, rows, row, cell, cols, col in piece_list(u, SHIFT_OUT):
                    sp.dma_start(out[unit[0], row:row + rows, col * C:(col + cols) * C],
                                 xr[lane:lane + rows, u, cell * C:(cell + cols) * C]
                                 ).then_inc(stored[u], 16)

            def prologue():
                for dst, src in ((g_sb[:, :, :].rearrange("p a b -> p (a b)")[:, 0:packed.shape[1]], packed),
                                 (ident[:, :], consts[:, 0:128]), (cst[:, :], consts[:, 128:147]),
                                 (w2_sb[:, :, :], w2),
                                 (wp_sb[:, :, :], wp)):
                    sp.dma_start(dst, src).then_inc(s_const, 16)
                for u in range(UPI):
                    load_a((0, u), u, first=True)
                for u in range(UPI):
                    load_r((0, u), u, first=True)

            def step(f, a, u):
                last_image = isinstance(f[0], int) and f[0] == B - 1
                if not last_image:
                    load_a((f[0], f[1] + UPI), u)
                store(f, u)
                if not last_image:
                    load_r((f[0], f[1] + UPI), u)

            schedule(sp, step, prologue)
            for u in range(UPI):
                sp.wait_ge(stored[u], 16 * len(piece_list(u, SHIFT_OUT)) * B)

        @block.gpsimd
        def _(pool):
            nc.gpsimd.memset(k_bd[:, :, :, :], 0.0).then_inc(s_zero, 1)
            nc.gpsimd.memset(v_bd[:, :, :], 0.0).then_inc(s_zero, 1)
            nc.gpsimd.memset(p_sb[:, :, :, :], 0.0).then_inc(s_zero, 1)

            def norm1(a):
                u = a[1] % UPI
                pool.wait_ge(var1_done, at(a, 1, 1))
                nc.gpsimd.tensor_tensor(rstd1[:, :], ve1[:, :], minus_half[0:LANES, :].broadcast_to([LANES, W]),
                                        ALU.pow).then_inc(rstd1_done, 1)
                if not first(a):
                    pool.wait_ge(t1_done, at(a, N_T1))
                wide = [LANES, W, C]
                nc.gpsimd.tensor_tensor(xn1[:, :, :], xa[:, u, :].rearrange("p (t c) -> p t c", c=C),
                                        mv1[:, :, 0:1].broadcast_to(wide), ALU.subtract
                                        ).then_inc(centre1_done, 1)
                pool.wait_ge(rstd1_done, at(a, 1, 1))
                pool.wait_ge(centre1_done, at(a, 1, 1))
                nc.gpsimd.tensor_tensor(xn1[:, :, :], xn1[:, :, :], rstd1[:, :].unsqueeze(2).broadcast_to(wide),
                                        ALU.mult).then_inc(norm1_done, 1)

            def rsqrt2(f):
                pool.wait_ge(var2_done, at(f, 1, 1))
                nc.gpsimd.tensor_tensor(rstd2[:, :], ve2[:, :], minus_half[0:LANES, :].broadcast_to([LANES, W]),
                                        ALU.pow).then_inc(rstd2_done, 1)

            def normalise_p(a):
                for n in range(8):
                    p = p_sb[0:SPAN, n % 2, :, 0:WW]
                    pool.wait_ge(rec_done, at(a, N_S, n + 1))
                    nc.gpsimd.tensor_tensor(p, p, s_rec[:, :].unsqueeze(2).broadcast_to([SPAN, HEADS, WW]),
                                            ALU.mult).then_inc(pnorm_done, 1)

            def prologue():
                pool.wait_ge(s_ready, 1)
                norm1((0, 0))
                norm1((0, 1))
                normalise_p((0, 0))

            def step(f, a, u):
                rsqrt2(f)
                if a is not None and not last(a):
                    norm1((a[0], a[1] + 1))
                if a is not None:
                    normalise_p(a)

            schedule(pool, step, prologue)

        @block.scalar
        def _(act):
            def x1_high(a):
                for k, (j0, n) in enumerate(((0, 4), (4, 3))):
                    act.wait_ge(t1_done, at(a, N_T1, k + 1))
                    src = bank[2 + k][0:C, 0:n * LANES].rearrange("p (j h w r) -> p h j w r", h=2, w=NW, r=W)
                    dst = windows(x1_hi[0:C, :])
                    for half in range(2):
                        nc.scalar.activation(dst[:, half, :, j0:j0 + n, :].rearrange("p w j r -> p j w r"),
                                             src[:, half], ACT.Copy).then_inc(x1hi_done, 1)

            def v_second(a):
                for k in range(2):
                    act.wait_ge(v_done, at(a, N_V, k + 1))
                    for odd in range(2):
                        nc.scalar.activation(v_dst(k, 1, odd), v_src(k, 1, odd), ACT.Copy,
                                             scale=1.0 / WSCALE).then_inc(vact_done, 1)

            def qk_split(a, t):
                kind = (t // GROUPS) % 2
                act.wait_ge(qk_done, at(a, N_QK, t + 1))
                if t >= 2:
                    act.wait_ge(stack_done, at(a, N_QK, t - 1))
                elif not first(a):
                    act.wait_ge(stack_done, at(a, N_QK))
                nc.scalar.activation(split[:, t % 2, :], bank[t % 2][:, 0:STRIP], ACT.Copy,
                                     scale=qk_col[kind]).then_inc(split_done, 1)

            def x2_high(f):
                for k, (j0, n) in enumerate(((0, 4), (4, 3))):
                    act.wait_ge(t2_done, at(f, N_T2, k + 1))
                    nc.scalar.activation(x2_hi[0:C, j0 * LANES:(j0 + n) * LANES],
                                         bank[5 + k][0:C, 0:n * LANES], ACT.Copy).then_inc(x2hi_done, 1)

            def gate_exp(f):
                act.wait_ge(router, at(f, N_ROUTER, 2))
                nc.scalar.activation(gexp[:, :, :], gsub[:, :, :], ACT.Exp,
                                     scale=1.0 / WSCALE).then_inc(gexp_done, 1)

            def gelus(f, k0):
                for k in range(k0, k0 + 3):
                    chunk, half = k // 2, k % 2
                    act.wait_ge(h_done, at(f, N_H, k + 1))
                    nc.scalar.activation(g_sb[:, chunk, half * STRIP:(half + 1) * STRIP],
                                         bank[5 + k % 2][:, 0:STRIP], ACT.Gelu,
                                         scale=1.0 / WSCALE).then_inc(gelu_done, 1)

            def exps(a, n):
                act.wait_ge(sub_done, at(a, N_S, n + 1))
                if n >= 2:
                    act.wait_ge(pt_done, at(a, N_PT, 2 * (n - 1)))
                elif not first(a):
                    act.wait_ge(pt_done, at(a, N_PT))
                nc.scalar.activation(p_sb[0:SPAN, n % 2, :, 0:WW], s_sub[:, :, 0:WW], ACT.Exp).then_inc(exp_done, 1)

            def copy_pt(a, n):
                act.wait_ge(pt_done, at(a, N_PT, 2 * n + 1))
                nc.scalar.activation(
                    pt_sb[0:SPAN, 0:4, :].rearrange("p h (s q) -> p h s q", s=2),
                    bank[2][0:SPAN, :].rearrange("p (h s q) -> p h s q", h=4, s=2)[:, :, :, 0:WW],
                    ACT.Copy).then_inc(pta_done, 1)

            def save_o(a, n):
                half, wr = n // 4, 2 * (n % 4)
                act.wait_ge(o_done, at(a, N_O, n + 1))
                if n == 0 and not first(a):
                    act.wait_ge(proj_done, at(a, N_PROJ))
                dst = o_sb[0:C, :, :].rearrange("p b (c h r) -> p b c h r", c=W, h=2)
                nc.scalar.activation(dst[:, :, :, half, W * wr:W * (wr + 2)],
                                     ps_o[0:C, 0:4 * WW].rearrange("p (b c r) -> p b c r", b=2, c=W),
                                     ACT.Copy).then_inc(o_saved, 1)

            def pairs(a):
                exps(a, 0)
                for n in range(8):
                    if n < 7:
                        exps(a, n + 1)
                    if n:
                        save_o(a, n - 1)
                    copy_pt(a, n)
                save_o(a, 7)

            def prologue():
                act.wait_ge(s_ready, 1)
                x1_high((0, 0))
                v_second((0, 0))
                for t in range(12):
                    qk_split((0, 0), t)
                pairs((0, 0))

            def step(f, a, u):
                if a is not None:
                    x1_high(a)
                    v_second(a)
                    for t in range(4):
                        qk_split(a, t)
                x2_high(f)
                for t in range(4, 12):
                    if a is not None:
                        qk_split(a, t)
                    gelus(f, 3 * (t - 4))
                gate_exp(f)
                if a is not None:
                    pairs(a)

            schedule(act, step, prologue)

        @block.vector
        def _(dve):
            fills = [0]

            def fill(ins):
                fills[0] += 1
                ins.then_inc(s_fill, 1)
                dve.wait_ge(s_fill, fills[0])

            V = nc.vector

            def setup():
                raw = g_sb[:, :, :].rearrange("p a b -> p (a b)")
                offs, o = {}, 0
                for name, n in SETUP:
                    offs[name] = raw[:, o:o + n]
                    o += n
                dve.wait_ge(s_const, 16 * N_CONST)
                dve.wait_ge(s_zero, 3)
                fill(V.tensor_copy(sel16[:, :], offs["sel"]))
                fill(V.tensor_copy(selB16[:, :], offs["selB"]))
                fill(V.tensor_copy(ul16[:, :], offs["ul"]))
                for src, hi, lo in (("wqk", wqk_hi, wqk_lo), ("wv", wv_hi, wv_lo),
                                    ("wg", wg_hi, wg_lo), ("w1", w1_hi, w1_lo)):
                    fill(V.tensor_scalar(hi[:, :], offs[src], WSCALE, None, ALU.mult))
                    fill(V.scalar_tensor_tensor(out=lo[:, :], in0=offs[src], scalar=WSCALE, in1=hi[:, :],
                                                op0=ALU.mult, op1=ALU.subtract))
                tmp = x1_hi[:, 0:384]
                fill(V.tensor_copy(tmp, offs["b2"]))
                fill(V.memset(b2_16[:, :], 0.0))
                fill(V.tensor_copy(b2_16[0:1, :], tmp[0:1, :]))
                fill(V.tensor_tensor(b2_16[32:33, :], offs["b2"][32:33, :], tmp[32:33, :], ALU.subtract))
                fill(V.memset(ones16[:, :], 1.0))
                tmp = x1_hi[:, 0:HEADS * WW]
                fill(V.tensor_copy(tmp, offs["rel"]))
                for v in range(2):
                    fill(V.tensor_tensor(bias16[NB:128, v, :], offs["rel"][NB:128, :], tmp[NB:128, :],
                                         ALU.subtract))
                fill(V.tensor_copy(bias16[0:NB, 0, :], tmp[0:NB, :]))
                fill(V.tensor_tensor(bias16[0:NB, 1, :], offs["rel"][0:NB, :], offs["lr"][0:NB, :], ALU.add))
                fill(V.memset(o_sb[C:128, :, :], 0.0))
                fill(V.memset(o_sb[C:C + 1, 0, :], 1.0))
                fill(V.memset(x1_hi[:, :], 0.0))
                fill(V.memset(x1_lo[:, :], 0.0))
                for hi, lo in ((x1_hi, x1_lo), (x2_hi, x2_lo)):
                    fill(V.memset(hi[ONES_ROW:128, :], 0.0))
                    fill(V.memset(hi[ONES_ROW:ONES_ROW + 1, :], 1.0))
                    fill(V.memset(lo[ONES_ROW:128, :], 0.0))
                V.memset(s_sub[:, :, :], 0.0).then_inc(s_ready, 1)
                dve.wait_ge(s_ready, 1)

            def ln1_stats(a):
                u = a[1] % UPI
                per = 16 * len(piece_list(u, SHIFT_IN))
                dve.wait_ge(xa_in[u], a[0] * per + (a[1] // UPI + 1) * per)
                if not first(a):
                    dve.wait_ge(norm1_done, at(a, 1))
                for t in range(W):
                    V.bn_stats(stat1[:, t, :], xa[:, u, t * C:(t + 1) * C]).then_inc(stat1_done, 1)
                dve.wait_ge(stat1_done, at(a, W, W))
                V.memset(mark[:, :], 0.0)
                for t in range(W):
                    V.bn_aggr(mv1[:, t, :], stat1[:, t, :]).then_inc(aggr1_done, 1)
                dve.wait_ge(aggr1_done, at(a, W, W))
                V.tensor_scalar(ve1[:, :], mv1[:, :, 1], EPS_C, None, ALU.add).then_inc(var1_done, 1)

            def x1_low(a):
                dst, hi = windows(x1_lo[0:C, :]), windows(x1_hi[0:C, :])
                for k, (j0, n) in enumerate(((0, 4), (4, 3))):
                    src = bank[2 + k][0:C, 0:n * LANES].rearrange("p (j h w r) -> p h j w r", h=2, w=NW, r=W)
                    for half in range(2):
                        dve.wait_ge(x1hi_done, at(a, N_XHI, 2 * k + 2))
                        V.tensor_tensor(dst[:, half, :, j0:j0 + n, :].rearrange("p w j r -> p j w r"),
                                        src[:, half],
                                        hi[:, half, :, j0:j0 + n, :].rearrange("p w j r -> p j w r"),
                                        ALU.subtract).then_inc(x1lo_done, 1)

            def v_first(a):
                for k in range(2):
                    dve.wait_ge(v_done, at(a, N_V, k + 1))
                    for odd in range(2):
                        V.tensor_scalar(v_dst(k, 0, odd), v_src(k, 0, odd), 1.0 / WSCALE, None, ALU.mult
                                        ).then_inc(vdve_done, 1)

            def qk_stack(a, t):
                half, kind, g = t // 6, (t // GROUPS) % 2, t % GROUPS
                scale = (QSCALE if kind == 0 else 1.0) / WSCALE
                dst = q_st[:, g, half * STRIP:(half + 1) * STRIP] if kind == 0 else k_st[:, t % 2, :]
                if kind:
                    before = K_ST_USED[half * GROUPS + g]
                    if before or not first(a):
                        dve.wait_ge(kbd_done, at(a, 6 * GH, before * GH))
                dve.wait_ge(split_done, at(a, N_QK, t + 1))
                V.scalar_tensor_tensor(out=dst, in0=bank[t % 2][:, 0:STRIP], scalar=scale,
                                       in1=split[:, t % 2, :], op0=ALU.mult, op1=ALU.subtract
                                       ).then_inc(stack_done, 1)
                if kind:
                    dve.wait_ge(stack_done, at(a, N_QK, t + 1))
                    for j in range(GH):
                        rows = slice(32 * j, 32 * j + 32)
                        V.tensor_copy(k_bd[rows, half * GROUPS + g, j, :], k_st[rows, t % 2, :]
                                      ).then_inc(kbd_done, 1)

            def softmax_pair(a, n):
                scores = ps_s[0:SPAN, 0:HEADS * NB].rearrange("p (h k) -> p h k", k=NB)[:, :, 0:WW]
                dve.wait_ge(s_done, at(a, N_S, n + 1))
                V.tensor_reduce(s_max[:, :], scores, AX.X, ALU.max).then_inc(max_done, 1)
                dve.wait_ge(max_done, at(a, N_S, n + 1))
                V.tensor_tensor(s_sub[:, :, 0:WW], scores,
                                s_max[:, :].unsqueeze(2).broadcast_to([SPAN, HEADS, WW]),
                                ALU.subtract).then_inc(sub_done, 1)

            def sums(a, n):
                dve.wait_ge(exp_done, at(a, N_S, n + 1))
                if n or not first(a):
                    dve.wait_ge(pnorm_done, at(a, N_S, n))
                V.tensor_reduce(s_sum[:, :], p_sb[0:SPAN, n % 2, :, 0:WW], AX.X, ALU.add).then_inc(sum_done, 1)
                dve.wait_ge(sum_done, at(a, N_S, n + 1))
                V.reciprocal(s_rec[:, :], s_sum[:, :]).then_inc(rec_done, 1)

            def copy_pt(a, n):
                dve.wait_ge(pt_done, at(a, N_PT, 2 * n + 2))
                V.tensor_copy(pt_sb[0:SPAN, 4:6, :].rearrange("p h (s q) -> p h s q", s=2),
                              bank[3][0:SPAN, 0:256].rearrange("p (h s q) -> p h s q", h=2, s=2)[:, :, :, 0:WW]
                              ).then_inc(ptb_done, 1)

            def residual(f, u):
                per = 16 * len(piece_list(u, SHIFT_OUT))
                dve.wait_ge(xr_in[u], f[0] * per + per)
                for k, (j0, n) in enumerate(((0, 4), (4, 3))):
                    dve.wait_ge(proj_done, at(f, N_PROJ, k + 1))
                    slot = xr[:, u, j0 * C:(j0 + n) * C]
                    V.tensor_tensor(slot, bank[6 + k][0:LANES, 0:n * C], slot, ALU.add).then_inc(res_done, 1)

            def ln2_stats(f, u):
                for t in range(W):
                    dve.wait_ge(res_done, at(f, 2, 1 + t // 4))
                    V.bn_stats(stat2[:, t, :], xr[:, u, t * C:(t + 1) * C]).then_inc(stat2_done, 1)
                dve.wait_ge(stat2_done, at(f, W, W))
                V.memset(mark[:, :], 0.0)
                for t in range(W):
                    V.bn_aggr(mv2[:, t, :], stat2[:, t, :]).then_inc(aggr2_done, 1)
                dve.wait_ge(aggr2_done, at(f, W, W))
                V.tensor_scalar(ve2[:, :], mv2[:, :, 1], EPS_T, None, ALU.add).then_inc(var2_done, 1)

            def ln2_norm(f, u):
                dve.wait_ge(rstd2_done, at(f, 1, 1))
                for t in range(W):
                    V.tensor_scalar(xn2[:, t, :], xr[:, u, t * C:(t + 1) * C], mv2[:, t, 0:1],
                                    rstd2[:, t:t + 1], ALU.subtract, ALU.mult).then_inc(norm2_done, 1)

            def x2_low(f):
                for k, (j0, n) in enumerate(((0, 4), (4, 3))):
                    cols = slice(j0 * LANES, (j0 + n) * LANES)
                    dve.wait_ge(x2hi_done, at(f, 2, k + 1))
                    V.tensor_tensor(x2_lo[0:C, cols], bank[5 + k][0:C, 0:n * LANES], x2_hi[0:C, cols],
                                    ALU.subtract).then_inc(x2lo_done, 1)

            def router_a(f):
                sc = bank[7][0:LANES, 0:W * EXPERTS].rearrange("p (t e) -> p t e", e=EXPERTS)
                dve.wait_ge(gate_done, at(f, 1, 1))
                V.tensor_reduce(gmax[:, :], sc, AX.X, ALU.max).then_inc(router, 1)
                dve.wait_ge(router, at(f, N_ROUTER, 1))
                V.tensor_tensor(gsub[:, :, :], sc, gmax[:, :].unsqueeze(2).broadcast_to([LANES, W, EXPERTS]),
                                ALU.subtract).then_inc(router, 1)

            def router_b(f):
                k = [2]

                def link(ins):
                    k[0] += 1
                    ins.then_inc(router, 1)
                    dve.wait_ge(router, at(f, N_ROUTER, k[0]))

                ge = gexp[:, :, :]
                mine = ge.rearrange("p t e -> p (t e)").unsqueeze(2).broadcast_to([LANES, W * EXPERTS, EXPERTS])
                mine = mine.rearrange("p (t e) f -> p t e f", e=EXPERTS)
                other = ge.unsqueeze(2).broadcast_to([LANES, W, EXPERTS, EXPERTS])
                gt4 = ggt[:, :, :].rearrange("p (t e) f -> p t e f", e=EXPERTS)
                eq4 = geq[:, :, :].rearrange("p (t e) f -> p t e f", e=EXPERTS)
                dve.wait_ge(gexp_done, at(f, 1, 1))
                V.tensor_tensor(gt4, other, mine, ALU.is_gt).then_inc(router, 1)
                k[0] += 1
                link(V.tensor_tensor(eq4, other, mine, ALU.is_equal))
                link(V.tensor_tensor(eq4, eq4, tie.unsqueeze(1).broadcast_to([LANES, W, EXPERTS, EXPERTS]),
                                     ALU.mult))
                link(V.tensor_tensor(ggt[:, :, :], ggt[:, :, :], geq[:, :, :], ALU.add))
                link(V.tensor_reduce(rank[:, :], ggt[:, :, :], AX.X, ALU.add))
                link(V.scalar_tensor_tensor(out=gsel[:, :, :].rearrange("p t e -> p (t e)"), in0=rank[:, :],
                                            scalar=1.5, in1=ge.rearrange("p t e -> p (t e)"),
                                            op0=ALU.is_lt, op1=ALU.mult))
                V.tensor_reduce(gtot[:, :], ge, AX.X, ALU.add).then_inc(router, 1)
                k[0] += 1
                link(V.tensor_reduce(gden[:, :], gsel[:, :, :], AX.X, ALU.add))
                link(V.scalar_tensor_tensor(out=gden[:, :], in0=gtot[:, :], scalar=1e-9, in1=gden[:, :],
                                            op0=ALU.mult, op1=ALU.add))
                link(V.reciprocal(gden[:, :], gden[:, :]))
                assert k[0] == N_ROUTER
                V.tensor_tensor(gate[:, :].rearrange("p (t e) -> p t e", e=EXPERTS), gsel[:, :, :],
                                gden[:, :].unsqueeze(2).broadcast_to([LANES, W, EXPERTS]),
                                ALU.mult).then_inc(gate_ready, 1)
                dve.wait_ge(gate_ready, at(f, 1, 1))

            def combine(f, u, j):
                slot = xr[:, u, j * C:(j + 1) * C]
                dve.wait_ge(y_done, at(f, N_Y, j + 1))
                for e in range(EXPERTS):
                    V.scalar_tensor_tensor(out=slot, in0=bank[7][0:LANES, e * C:(e + 1) * C],
                                           scalar=gate[:, j * EXPERTS + e:j * EXPERTS + e + 1], in1=slot,
                                           op0=ALU.mult, op1=ALU.add).then_inc(comb_done, 1)
                    dve.wait_ge(comb_done, at(f, N_COMB, j * EXPERTS + e + 1))

            def prologue():
                setup()
                ln1_stats((0, 0))
                x1_low((0, 0))
                ln1_stats((0, 1))
                v_first((0, 0))
                for t in range(12):
                    qk_stack((0, 0), t)
                softmax_pair((0, 0), 0)
                for n in range(8):
                    sums((0, 0), n)
                    if n < 7:
                        softmax_pair((0, 0), n + 1)
                    copy_pt((0, 0), n)

            def step(f, a, u):
                if a is not None:
                    x1_low(a)
                residual(f, u)
                ln2_stats(f, u)
                if a is not None:
                    v_first(a)
                    for t in range(2):
                        qk_stack(a, t)
                ln2_norm(f, u)
                if a is not None:
                    for t in range(2, 4):
                        qk_stack(a, t)
                x2_low(f)
                router_a(f)
                if a is not None:
                    for t in range(4, 12):
                        qk_stack(a, t)
                    if not last(a):
                        ln1_stats((a[0], a[1] + 1))
                    softmax_pair(a, 0)
                router_b(f)
                for n in range(8):
                    if a is not None:
                        sums(a, n)
                        if n < 7:
                            softmax_pair(a, n + 1)
                    if n < 7:
                        combine(f, u, n)
                    if a is not None:
                        copy_pt(a, n)

            schedule(dve, step, prologue)

        @block.tensor
        def _(pe):
            T = nc.tensor

            def three(outp, lhs_hi, lhs_lo, rhs_hi, rhs_lo, start=True):
                T.matmul(outp, lhs_hi, rhs_hi, start=start, stop=False, skip_group_check=True)
                T.matmul(outp, lhs_hi, rhs_lo, start=False, stop=False, skip_group_check=True)
                return T.matmul(outp, lhs_lo, rhs_hi, start=False, stop=True, skip_group_check=True)

            def transpose1(a):
                pe.wait_ge(norm1_done, at(a, 1, 1))
                for k, (j0, n) in enumerate(((0, 4), (4, 3))):
                    for j in range(n):
                        ins = T.transpose(bank[2 + k][0:C, j * LANES:(j + 1) * LANES], xn1[:, j0 + j, :],
                                          ident[0:LANES, 0:LANES])
                    ins.then_inc(t1_done, 1)

            def values(a):
                pe.wait_ge(x1lo_done, at(a, N_X1LO, N_X1LO))
                if not first(a):
                    pe.wait_ge(o_saved, at(a, N_O))
                for k in range(2):
                    for w in range(4):
                        xc = slice((k * 4 + w) * 2 * WPAD, (k * 4 + w + 1) * 2 * WPAD)
                        ins = three(bank[3 + k][:, w * C:(w + 1) * C], x1_hi[:, xc], x1_lo[:, xc],
                                    wv_hi[:, :], wv_lo[:, :])
                    ins.then_inc(v_done, 1)

            def qk(a, t):
                half, col = t // 6, (t % 6) * 128
                if t >= 2:
                    pe.wait_ge(stack_done, at(a, N_QK, t - 1))
                elif not first(a):
                    pe.wait_ge(sub_done, at(a, N_S))
                three_w(bank[t % 2][:, 0:STRIP], wqk_hi[:, col:col + 128], wqk_lo[:, col:col + 128],
                        strip(x1_hi, half), strip(x1_lo, half)).then_inc(qk_done, 1)

            def strip(t, half):
                return t.rearrange("p (h w k) -> p h w k", h=2, k=WPAD)[:, half, :, 0:WW]

            def three_w(outp, w_hi, w_lo, x_hi, x_lo):
                return three(outp, w_hi, w_lo, x_hi, x_lo)

            def scores(a, n):
                half, wr = n // 4, 2 * (n % 4)
                if n == 0:
                    pe.wait_ge(stack_done, at(a, N_QK, N_QK))
                    pe.wait_ge(kbd_done, at(a, 6 * GH, 6 * GH))
                else:
                    pe.wait_ge(sub_done, at(a, N_S, n))
                variant = 1 if half == 1 and a[1] % UPI == UPI - 1 else 0
                s3 = ps_s[0:SPAN, 0:HEADS * NB].rearrange("p (h k) -> p h k", k=NB)
                for h0, h1 in ((0, 8), (8, 12)):
                    T.matmul(s3[:, h0:h1, 0:WW], sel16[:, :], bias16[:, variant, h0 * WW:h1 * WW],
                             start=True, stop=False, skip_group_check=True)
                    if wr == NW - 2:
                        T.matmul(s3[:, h0:h1, 0:WW], selB16[:, :], ul16[:, h0 * WW:h1 * WW],
                                 start=False, stop=False, skip_group_check=True)
                for s in range(2):
                    x0 = half * STRIP + (wr + s) * WW
                    k0 = (wr + s) * WW
                    part = ps_s[NB * s:NB * s + WW, 0:HEADS * NB].rearrange("p (h k) -> p h k", k=NB)
                    for g in range(GROUPS):
                        ins = T.matmul(part[:, g * GH:(g + 1) * GH, 0:WW], q_st[:, g, x0:x0 + WW],
                                       k_bd[:, half * GROUPS + g, :, k0:k0 + WW],
                                       start=False, stop=True, skip_group_check=True)
                ins.then_inc(s_done, 1)

            def transpose_p(a, n):
                if n == 0:
                    pe.wait_ge(vact_done, at(a, N_XV, N_XV))
                    pe.wait_ge(vdve_done, at(a, N_XV, N_XV))
                pe.wait_ge(pnorm_done, at(a, N_S, n + 1))
                for p in range(PAIRS):
                    ins = T.transpose(bank[2 + p // 4][0:SPAN, (p % 4) * 128:(p % 4) * 128 + SPAN],
                                      p_sb[0:SPAN, n % 2, 2 * p:2 * p + 2, :].rearrange("p h k -> p (h k)")[:, 0:SPAN],
                                      ident[0:SPAN, 0:SPAN])
                    if p in (3, 5):
                        ins.then_inc(pt_done, 1)

            def attend(a, n):
                half, wr = n // 4, 2 * (n % 4)
                pe.wait_ge(pta_done, at(a, N_S, n + 1))
                pe.wait_ge(ptb_done, at(a, N_S, n + 1))
                if n:
                    pe.wait_ge(o_saved, at(a, N_O, n))
                for s in range(2):
                    win = half * NW + wr + s
                    for p in range(PAIRS):
                        rows = slice(32 * (p % 3), 32 * (p % 3) + 32)
                        o = ps_o[rows, (p // 3) * 98:(p // 3) * 98 + 98]
                        o = o.rearrange("p (c s r) -> p c s r", c=W, s=2)[:, :, s, :]
                        ins = T.matmul(o, v_bd[0:SPAN, win * PAIRS + p, :], pt_sb[0:SPAN, p, s * WW:(s + 1) * WW],
                                       start=True, stop=True, skip_group_check=True)
                ins.then_inc(o_done, 1)

            def project(f):
                pe.wait_ge(o_saved, at(f, N_O, N_O))
                for k, (j0, n) in enumerate(((0, 4), (4, 3))):
                    for j in range(n):
                        for blk in range(2):
                            ins = T.matmul(bank[6 + k][0:LANES, j * C:(j + 1) * C],
                                           o_sb[:, blk, (j0 + j) * LANES:(j0 + j + 1) * LANES],
                                           wp_sb[:, blk, :], start=(blk == 0), stop=(blk == 1))
                    ins.then_inc(proj_done, 1)

            def transpose2(f):
                pe.wait_ge(norm2_done, at(f, W, W))
                for k, (j0, n) in enumerate(((0, 4), (4, 3))):
                    for j in range(n):
                        ins = T.transpose(bank[5 + k][0:C, j * LANES:(j + 1) * LANES], xn2[:, j0 + j, :],
                                          ident[0:LANES, 0:LANES])
                    ins.then_inc(t2_done, 1)

            def gate_scores(f):
                pe.wait_ge(x2lo_done, at(f, 2, 2))
                for j in range(W):
                    cols = slice(j * LANES, (j + 1) * LANES)
                    ins = three(bank[7][0:LANES, j * EXPERTS:(j + 1) * EXPERTS], x2_hi[:, cols],
                                x2_lo[:, cols], wg_hi[:, :], wg_lo[:, :])
                ins.then_inc(gate_done, 1)

            def hidden(f, k0):
                for k in range(k0, k0 + 3):
                    chunk, half = k // 2, k % 2
                    if k >= 2:
                        pe.wait_ge(gelu_done, at(f, N_H, k - 1))
                    wc = slice(chunk * 128, (chunk + 1) * 128)
                    xc = slice(half * STRIP, (half + 1) * STRIP)
                    three_w(bank[5 + k % 2][:, 0:STRIP], w1_hi[:, wc], w1_lo[:, wc],
                            x2_hi[:, xc], x2_lo[:, xc]).then_inc(h_done, 1)

            def experts(f, j):
                if j == 0:
                    pe.wait_ge(gelu_done, at(f, N_H, N_H))
                    pe.wait_ge(router, at(f, N_ROUTER, 2))
                else:
                    pe.wait_ge(comb_done, at(f, N_COMB, j * EXPERTS))
                T.matmul(bank[7][0:LANES, 0:EXPERTS * C], ones16[:, :], b2_16[:, :],
                         start=True, stop=False, skip_group_check=True)
                for e in range(EXPERTS):
                    for c in range(CPE):
                        ins = T.matmul(bank[7][0:LANES, e * C:(e + 1) * C],
                                       g_sb[:, e * CPE + c, j * LANES:(j + 1) * LANES],
                                       w2_sb[:, e * CPE + c, :], start=False, stop=(c == CPE - 1),
                                       skip_group_check=True)
                ins.then_inc(y_done, 1)

            def prologue():
                pe.wait_ge(s_ready, 1)
                transpose1((0, 0))
                values((0, 0))
                for t in range(12):
                    qk((0, 0), t)
                scores((0, 0), 0)
                for n in range(9):
                    attention_slot((0, 0), n)

            def attention_slot(a, n, between=None):
                if n < 7:
                    scores(a, n + 1)
                if between:
                    between()
                if n:
                    attend(a, n - 1)
                if n < 8:
                    transpose_p(a, n)

            def step(f, a, u):
                if a is not None:
                    transpose1(a)
                project(f)
                if a is not None:
                    values(a)
                    for t in range(4):
                        qk(a, t)
                transpose2(f)
                for t in range(4, 12):
                    if a is not None:
                        qk(a, t)
                    if t == 4:
                        gate_scores(f)
                    hidden(f, 3 * (t - 4))
                if a is not None:
                    scores(a, 0)
                for n in range(9):
                    tile = (lambda: experts(f, n)) if n < 7 else None
                    if a is not None:
                        attention_slot(a, n, tile)
                    elif tile:
                        tile()

            schedule(pe, step, prologue)


def _rows(a, rows=128):
    out = np.zeros((rows,) + a.shape[1:], a.dtype)
    out[:a.shape[0]] = a
    return out


def _layout(w_qkv, b_qkv, w_proj, b_proj, rel_table, gate_w, gate_b, w1, b1, w2, b2):
    f = np.float32
    wb = np.concatenate([w_qkv.T, b_qkv[None]], 0)
    qk = wb[:, :2 * C].reshape(97, 2, HEADS, 1, HD)
    wqk = np.zeros((97, 2, HEADS, 4, HD), f)
    wqk[:, :, :, 0:3] = qk
    wqk = wqk.reshape(97, 768)
    wv = wb[:, 2 * C:].reshape(97, PAIRS, 2, HD).transpose(0, 2, 1, 3).reshape(97, C)
    wg = np.concatenate([gate_w, gate_b[None]], 0)
    w1b = np.concatenate([w1.transpose(1, 0, 2).reshape(C, EXPERTS * HID), b1.reshape(1, -1)], 0)
    b2r = np.zeros((128, EXPERTS * C), f)
    b2r[0] = b2r[32] = b2.reshape(-1)
    col, row = np.arange(WW) // W, np.arange(WW) % W
    idx = (row[:, None] - row[None] + W - 1) * (2 * W - 1) + (col[:, None] - col[None] + W - 1)
    rel = np.zeros((128, HEADS, WW), f)
    rel[0:WW] = rel[NB:SPAN] = rel_table[idx].transpose(0, 2, 1)
    late = lambda v: v >= W - W // 2
    lr, ul = np.zeros((128, HEADS, WW), f), np.zeros((128, HEADS, WW), f)
    lr[0:WW] = np.where(late(col)[:, None] != late(col)[None], MASKED, 0.0)[:, None, :]
    ul[0:WW] = np.where(late(row)[:, None] != late(row)[None], MASKED, 0.0)[:, None, :]
    sel, selB = np.zeros((128, SPAN), f), np.zeros((128, SPAN), f)
    q = np.arange(WW)
    for k0 in (0, NB):
        for m0 in (0, NB):
            sel[k0 + q, m0 + q] = 1.0
    selB[q, NB + q] = 1.0
    parts = {"wqk": _rows(wqk), "wv": _rows(wv), "wg": _rows(wg), "w1": _rows(w1b), "b2": b2r,
             "rel": rel.reshape(128, -1), "lr": lr.reshape(128, -1), "ul": ul.reshape(128, -1),
             "sel": sel, "selB": selB}
    packed = np.concatenate([parts[name] for name, _ in SETUP], 1).astype(f)
    wp = np.zeros((2, 128, C), f)
    wp[:, 0:C].reshape(2, 3, 32, C)[:, :, 0:16] = w_proj.T.reshape(2, 3, 16, C)
    wp[0, C] = b_proj
    wp = np.ascontiguousarray(wp.transpose(1, 0, 2))
    w2p = np.ascontiguousarray(w2.reshape(EXPERTS, CPE, 128, C).transpose(2, 0, 1, 3).reshape(128, CHUNKS, C))
    consts = np.zeros((128, 147), f)
    consts[:, 0:128] = np.eye(128)
    rep = np.arange(128) % 32 // HD
    consts[:, 128] = np.where(rep == 2, QSCALE / WSCALE, 0.0)
    consts[:, 129] = np.where(rep == 1, 1.0 / WSCALE, 0.0)
    consts[:, 130] = -0.5
    e = np.arange(EXPERTS)
    consts[:, 131:147] = (e[None, :] < e[:, None]).astype(f).reshape(1, -1)
    return packed, w2p, wp, consts


def kernel(**inputs):
    import concourse.bacc as bacc
    from concourse.bass_utils import run_bass_kernel_spmd

    a = {k: np.asarray(v) for k, v in inputs.items()}
    c, g = "L0_conv_", "L0_ffn_"
    packed, w2, wp, consts = _layout(a[c + "w_qkv"], a[c + "b_qkv"], a[c + "w_proj"], a[c + "b_proj"],
                                     a[c + "rel_table"], a[g + "gate_w"], a[g + "gate_b"],
                                     a[g + "w1"], a[g + "b1"], a[g + "w2"], a[g + "b2"])
    arrays = {"x": np.ascontiguousarray(a["x"]).reshape(B, IMG, IMG * C), "packed": packed, "w2": w2,
              "wp": wp, "consts": consts}
    nc = bacc.Bacc("TRN2", target_bir_lowering=False, num_devices=1)
    aps = [nc.dram_tensor(n, v.shape, F32, kind="ExternalInput").ap() for n, v in arrays.items()]
    out = nc.dram_tensor("out", (B, IMG, IMG * C), F32, kind="ExternalOutput").ap()
    build(nc, *aps, out)
    r = run_bass_kernel_spmd(nc, [arrays], core_ids=[0])
    return r.results[0]["out"].reshape(B, IMG, IMG, C)
```

```python
from contextlib import ExitStack

import numpy as np

import concourse.bass as bass
from concourse import mybir

F32 = mybir.dt.float32
F16 = mybir.dt.float16
ALU = mybir.AluOpType
ACT = mybir.ActivationFunctionType
AX = mybir.AxisListType

B, IMG, C = 32, 56, 96
W = 7
WW = W * W
NW = IMG // W
HEADS, HD = 12, 8
PAIRS = HEADS // 2
GROUPS, GH = 3, 4
EXPERTS, HID = 4, 384
CHUNKS = EXPERTS * HID // 128
CPE = HID // 128
UPI = 4
STRIP = W * IMG
TOK = 2 * STRIP
LANES = 2 * IMG
NB = 64
SPAN = NB + WW
SHIFT_IN, SHIFT_OUT = 4, 3
WSCALE = 64.0
EPS_C, EPS_T = 1e-6, 1e-5
ONES_ROW = 96
MASKED = -60000.0


def at(unit, per_unit, k=0):
    m, c = unit
    return m * (UPI * per_unit) + (c * per_unit + k)


def first(unit):
    return isinstance(unit[0], int) and unit == (0, 0)


def last(unit):
    return isinstance(unit[0], int) and unit == (B - 1, UPI - 1)


def following(unit):
    return None if last(unit) else (unit[0], unit[1] + 1)


def hidden_part(k):
    return (k % 3, k // 3) if k < 6 else (k // 2, k % 2)


def piece_list(u, shift):
    out = []
    for half in range(2):
        c0 = (half * IMG // 2 + u * W + shift)
        runs = []
        n0 = min(W, max(0, IMG - c0))
        if n0:
            runs.append((0, n0, c0))
        if n0 < W:
            runs.append((n0, W - n0, (c0 + n0) % IMG))
        for r0, rows, row in ((0, IMG - shift, shift), (IMG - shift, shift, 0)):
            for cell, cols, col in runs:
                out.append((half * IMG + r0, rows, row, cell, cols, col))
    return out


TURNS = [(2 * b + s, e) for b in range(3) for e in range(EXPERTS) for s in range(2)]
TURNS = [TURNS[3 * g:3 * g + 3] for g in range(8)] + [[(W - 1, e) for e in range(EXPERTS)]]
GROUPS_AT = ((0, 1), (2,), (3,), (4,), (5,), (6,), (7,), (), ())
COMBINES_AT = ((0,), (1,), (2,), (3, 4), (5,), (6,), (), (7,))
T1_AT = 4
X1_LOW_AT = ((), (), (), (), (), (0, 1), (2, 3), ())
Y_BANK = (5, 7, 6, 5, 6, 7, 7, 7, 4)
B2_COLS = (2 * EXPERTS + 2) * C
N_T1, N_QK, N_V, N_S, N_PT, N_O = 2, 4, 2, 8, 16, 8
N_XV = 8
N_PROJ, N_T2, N_H, N_Y = 2, 2, 24, len(TURNS)
N_XHI, N_X1LO = 4, 4
N_COMB = 7 * EXPERTS
N_STACK = 16 * 3 * GROUPS
N_KBD = GROUPS * GH
QSCALE = HD ** -0.5
QK_SCALE = (QSCALE / WSCALE, 1.0 / WSCALE)

SETUP = (("wqk", 2 * C), ("wv", C), ("wg", EXPERTS), ("w1", CHUNKS * 128), ("b2", B2_COLS),
         ("rel", HEADS * WW), ("lr", HEADS * WW), ("ul", HEADS * WW), ("sel", SPAN), ("selB", SPAN))
N_CONST = 5


def build(nc, x, packed, w2, wp, consts, out):
    ctx = ExitStack()
    with ctx:
        def sb(name, shape, dt=F32):
            return ctx.enter_context(nc.sbuf_tensor(name, shape, dt))

        def sem(name):
            return ctx.enter_context(nc.semaphore(name))

        bank = [None] * 8
        ps_s = ctx.enter_context(nc.psum_tensor("ps_s", [128, 1024], F32))
        ps_t = ctx.enter_context(nc.psum_tensor("ps_t", [128, 1024], F32))
        ps_o = ctx.enter_context(nc.psum_tensor("ps_o", [128, 512], F32)) 
        ps_f = ctx.enter_context(nc.psum_tensor("ps_f", [128, 1536], F32))
        bank[0:2] = [ps_s[:, 0:512], ps_s[:, 512:1024]]
        bank[2:4] = [ps_t[:, 0:512], ps_t[:, 512:1024]]
        bank[4] = ps_o[:, :]
        bank[5:8] = [ps_f[:, k * 512:(k + 1) * 512] for k in range(3)]

        ident = sb("ident", [128, 128])
        cst = sb("cst", [128, GH + 2 + 16])
        head_rows = cst[0:C, 0:GH]
        minus_half = cst[:, 4:5]
        euler = cst[0:LANES, 5:6]
        tie = cst[0:LANES, 6:22].rearrange("p (e f) -> p e f", f=EXPERTS)
        sel16 = sb("sel16", [128, SPAN], F16)
        selB16 = sb("selB16", [128, SPAN], F16)
        ul16 = sb("ul16", [128, HEADS * WW], F16)
        bias16 = sb("bias16", [128, 2, HEADS * WW], F16)
        wqk_hi = sb("wqk_hi", [128, 2 * C], F16)
        wqk_lo = sb("wqk_lo", [128, 2 * C], F16)
        wv_hi = sb("wv_hi", [128, C], F16)
        wv_lo = sb("wv_lo", [128, C], F16)
        wg_hi = sb("wg_hi", [128, EXPERTS], F16)
        wg_lo = sb("wg_lo", [128, EXPERTS], F16)
        w1_hi = sb("w1_hi", [128, CHUNKS * 128], F16)
        w1_lo = sb("w1_lo", [128, CHUNKS * 128], F16)
        w2_sb = sb("w2_sb", [128, CHUNKS, C])
        wp_sb = sb("wp_sb", [128, 2, C])
        b2_16 = sb("b2_16", [128, B2_COLS], F16)
        ones16 = sb("ones16", [128, LANES], F16)

        xa = sb("xa", [LANES, UPI, W * C])
        stat1 = sb("stat1", [LANES, W, 6])
        tables = sb("tables", [1, 1])
        mark = sb("mark", [LANES, 1])
        mv1 = sb("mv1", [LANES, W, 2])
        ve1 = sb("ve1", [LANES, W])
        rstd1 = sb("rstd1", [LANES, W])
        xn1 = sb("xn1", [LANES, W, C])
        x1_hi = sb("x1_hi", [128, TOK], F16)
        x1_lo = sb("x1_lo", [128, TOK], F16)
        qk_hi = sb("qk_hi", [C, 2, TOK], F16)
        qk_lo = sb("qk_lo", [C, 2, TOK], F16)
        q_st = sb("q_st", [128, GROUPS, TOK], F16)
        k_st = sb("k_st", [C, GROUPS, TOK], F16)
        k_bd = sb("k_bd", [128, GROUPS, GH, TOK], F16)
        v_bd = sb("v_bd", [128, 16 * PAIRS, 32])
        s_max = sb("s_max", [SPAN, HEADS])
        s_sub = sb("s_sub", [SPAN, HEADS, NB])
        s_sum = sb("s_sum", [SPAN, HEADS])
        s_rec = sb("s_rec", [SPAN, HEADS])
        p_sb = sb("p_sb", [128, 2, HEADS, NB])
        pt_sb = sb("pt_sb", [128, PAIRS, 2 * WW])
        o_sb = sb("o_sb", [128, 2, TOK])

        xr = sb("xr", [LANES, UPI, W * C])
        stat2 = sb("stat2", [LANES, W, 6])
        mv2 = sb("mv2", [LANES, W, 2])
        ve2 = sb("ve2", [LANES, W])
        rstd2 = sb("rstd2", [LANES, W])
        xn2 = sb("xn2", [LANES, W, C])
        x2_hi = sb("x2_hi", [128, TOK + 16], F16)
        x2_lo = sb("x2_lo", [128, TOK + 16], F16)
        gmax = sb("gmax", [LANES, W])
        gsub = sb("gsub", [LANES, W, EXPERTS])
        gexp = sb("gexp", [LANES, W, EXPERTS])
        ggt = sb("ggt", [LANES, W * EXPERTS, EXPERTS])
        geq = sb("geq", [LANES, W * EXPERTS, EXPERTS])
        rank = sb("rank", [LANES, W * EXPERTS])
        gsel = sb("gsel", [LANES, W, EXPERTS])
        gtot = sb("gtot", [LANES, W])
        gden = sb("gden", [LANES, W])
        gate = sb("gate", [LANES, W * EXPERTS])
        g_sb = sb("g_sb", [128, CHUNKS, TOK])

        s_const = sem("s_const")
        s_zero = sem("s_zero")
        s_fill = sem("s_fill")
        s_ready = sem("s_ready")
        xa_in = [sem(f"xa_in{u}") for u in range(UPI)]
        xr_in = [sem(f"xr_in{u}") for u in range(UPI)]
        stored = [sem(f"stored{u}") for u in range(UPI)]
        t1_done, qk_done, v_done = sem("t1_done"), sem("qk_done"), sem("v_done")
        s_done, pt_done, o_done = sem("s_done"), sem("pt_done"), sem("o_done")
        proj_done, t2_done = sem("proj_done"), sem("t2_done")
        gate_done, h_done, y_done = sem("gate_done"), sem("h_done"), sem("y_done")
        x1hi_done, qkhi_done, exp_done = sem("x1hi_done"), sem("qkhi_done"), sem("exp_done")
        v_saved, pt_saved, o_saved = sem("v_saved"), sem("pt_saved"), sem("o_saved")
        x2hi_done, gexp_done, gelu_done = sem("x2hi_done"), sem("gexp_done"), sem("gelu_done")
        stat1_done, aggr1_done, var1_done = sem("stat1_done"), sem("aggr1_done"), sem("var1_done")
        rstd1_done, centre1_done, norm1_done = sem("rstd1_done"), sem("centre1_done"), sem("norm1_done")
        x1lo_done, qklo_done, kbd_done = sem("x1lo_done"), sem("qklo_done"), sem("kbd_done")
        q_in, k_in = sem("q_in"), sem("k_in")
        max_done, sub_done = sem("max_done"), sem("sub_done")
        sum_done, rec_done, pnorm_done = sem("sum_done"), sem("rec_done"), sem("pnorm_done")
        res_done = sem("res_done")
        stat2_done, aggr2_done, var2_done = sem("stat2_done"), sem("aggr2_done"), sem("var2_done")
        rstd2_done, centre2_done = sem("rstd2_done"), sem("centre2_done")
        norm2_done, x2lo_done = sem("norm2_done"), sem("x2lo_done")
        gate_ready = sem("gate_ready")
        router = sem("router")
        comb_done = sem("comb_done")

        N_ROUTER = 13

        def windows(t):
            return t.rearrange("p (h w c r) -> p h w c r", h=2, w=NW, c=W)

        def v_src(k, s, odd):
            src = bank[2 + k][NB * s:NB * s + WW, 0:4 * C].rearrange("p (n z) -> p n z", z=C)
            return src[:, :, 48 * odd:48 * odd + 48].rearrange("p n (h d) -> p n h d", d=HD)

        def v_dst(k, s, odd):
            dst = v_bd[NB * odd:NB * odd + WW, k * 48:(k + 1) * 48, HD * odd:HD * (odd + 1)]
            return dst.rearrange("p (n s h) d -> p n s h d", s=2, h=PAIRS)[:, :, s]

        def y_bank(g):
            return bank[Y_BANK[g]]

        h_bank = [bank[5], bank[7], bank[6]]

        block = ctx.enter_context(nc.Block())

        LOOPS = B - 1

        def schedule(eng, step, prologue):
            prologue()
            with eng.Fori(0, LOOPS) as m:
                for u in range(UPI):
                    with eng.register(f"image_{u}") as counter:
                        eng.reg_mov(counter, m)
                        image = eng.snap(counter)
                        step((image, u), (image, u + 1), (image, u + 2), u)
            for u in range(UPI):
                a = following((LOOPS, u))
                step((LOOPS, u), a, a and following(a), u)

        @block.sync
        def _(sp):
            def visit(unit, u):
                return (unit[0], (unit[1] - u) // UPI)

            def slot_at(unit, u, per, k):
                m, extra = visit(unit, u)
                return m * per + (extra * per + k)

            def load_a(unit, u, first=False):
                if not first:
                    sp.wait_ge(norm1_done, at((unit[0], unit[1] - UPI), 1, 1))
                img = unit[0] + unit[1] // UPI
                for lane, rows, row, cell, cols, col in piece_list(u, SHIFT_IN):
                    sp.dma_start(xa[lane:lane + rows, u, cell * C:(cell + cols) * C],
                                 x[img, row:row + rows, col * C:(col + cols) * C]
                                 ).then_inc(xa_in[u], 16)

            def load_r(unit, u, first=False):
                if not first:
                    n = 16 * len(piece_list(u, SHIFT_OUT))
                    sp.wait_ge(stored[u], slot_at((unit[0], unit[1] - UPI), u, n, n))
                img = unit[0] + unit[1] // UPI
                for lane, rows, row, cell, cols, col in piece_list(u, SHIFT_OUT):
                    sp.dma_start(xr[lane:lane + rows, u, cell * C:(cell + cols) * C],
                                 x[img, row:row + rows, col * C:(col + cols) * C]
                                 ).then_inc(xr_in[u], 16)

            def store(unit, u):
                sp.wait_ge(comb_done, at(unit, N_COMB, N_COMB))
                for lane, rows, row, cell, cols, col in piece_list(u, SHIFT_OUT):
                    sp.dma_start(out[unit[0], row:row + rows, col * C:(col + cols) * C],
                                 xr[lane:lane + rows, u, cell * C:(cell + cols) * C]
                                 ).then_inc(stored[u], 16)

            def build_stacks(unit):
                for kind, stack, parts, landed in ((1, k_st, (qk_hi, qk_lo, qk_hi), k_in),
                                                   (0, q_st, (qk_hi, qk_hi, qk_lo), q_in)):
                    sp.wait_ge(qkhi_done, at(unit, N_QK, 4 - 2 * kind))
                    sp.wait_ge(qklo_done, at(unit, N_QK, 4 - 2 * kind))
                    for g in range(GROUPS):
                        for r, part in enumerate(parts):
                            sp.dma_start(stack[32 * r:32 * r + 32, g, :],
                                         part[32 * g:32 * g + 32, kind, :]).then_inc(landed, 16)

            def prologue():
                for dst, src in ((g_sb[:, :, :].rearrange("p a b -> p (a b)")[:, 0:packed.shape[1]], packed),
                                 (ident[:, :], consts[:, 0:128]), (cst[:, :], consts[:, 128:150]),
                                 (w2_sb[:, :, :], w2),
                                 (wp_sb[:, :, :], wp)):
                    sp.dma_start(dst, src).then_inc(s_const, 16)
                for u in range(UPI):
                    load_a((0, u), u, first=True)
                for u in range(UPI):
                    load_r((0, u), u, first=True)
                build_stacks((0, 0))
                build_stacks((0, 1))

            def step(f, a, b, u):
                last_image = isinstance(f[0], int) and f[0] == B - 1
                if not last_image:
                    load_a((f[0], f[1] + UPI), u)
                if b is not None:
                    build_stacks(b)
                store(f, u)
                if not last_image:
                    load_r((f[0], f[1] + UPI), u)

            schedule(sp, step, prologue)
            for u in range(UPI):
                sp.wait_ge(stored[u], 16 * len(piece_list(u, SHIFT_OUT)) * B)

        @block.gpsimd
        def _(pool):
            nc.gpsimd.memset(k_bd[:, :, :, :], 0.0).then_inc(s_zero, 1)
            nc.gpsimd.memset(v_bd[:, :, :], 0.0).then_inc(s_zero, 1)
            nc.gpsimd.memset(p_sb[:, :, :, :], 0.0).then_inc(s_zero, 1)

            def norm1(a):
                u = a[1] % UPI
                pool.wait_ge(var1_done, at(a, 1, 1))
                nc.gpsimd.tensor_tensor(rstd1[:, :], ve1[:, :], minus_half[0:LANES, :].broadcast_to([LANES, W]),
                                        ALU.pow).then_inc(rstd1_done, 1)
                if not first(a):
                    pool.wait_ge(t1_done, at(a, N_T1))
                wide = [LANES, W, C]
                nc.gpsimd.tensor_tensor(xn1[:, :, :], xa[:, u, :].rearrange("p (t c) -> p t c", c=C),
                                        mv1[:, :, 0:1].broadcast_to(wide), ALU.subtract
                                        ).then_inc(centre1_done, 1)
                pool.wait_ge(rstd1_done, at(a, 1, 1))
                pool.wait_ge(centre1_done, at(a, 1, 1))
                nc.gpsimd.tensor_tensor(xn1[:, :, :], xn1[:, :, :], rstd1[:, :].unsqueeze(2).broadcast_to(wide),
                                        ALU.mult).then_inc(norm1_done, 1)

            def rsqrt2(f):
                for k, (j0, n) in enumerate(((0, 4), (4, 3))):
                    pool.wait_ge(var2_done, at(f, 2, k + 1))
                    nc.gpsimd.tensor_tensor(rstd2[:, j0:j0 + n], ve2[:, j0:j0 + n],
                                            minus_half[0:LANES, :].broadcast_to([LANES, n]),
                                            ALU.pow).then_inc(rstd2_done, 1)

            def gate_exp(f):
                n = W * EXPERTS
                pool.wait_ge(router, at(f, N_ROUTER, 3))
                nc.gpsimd.tensor_tensor(gexp[:, :, :].rearrange("p t e -> p (t e)"),
                                        euler.broadcast_to([LANES, n]),
                                        gsub[:, :, :].rearrange("p t e -> p (t e)"), ALU.pow
                                        ).then_inc(gexp_done, 1)

            def normalise_p(a):
                for n in range(8):
                    p = p_sb[0:SPAN, n % 2, :, 0:WW]
                    pool.wait_ge(rec_done, at(a, N_S, n + 1))
                    nc.gpsimd.tensor_tensor(p, p, s_rec[:, :].unsqueeze(2).broadcast_to([SPAN, HEADS, WW]),
                                            ALU.mult).then_inc(pnorm_done, 1)

            def prologue():
                pool.wait_ge(s_ready, 1)
                norm1((0, 0))
                norm1((0, 1))
                normalise_p((0, 0))
                rsqrt2((0, 0))
                gate_exp((0, 0))

            def step(f, a, b, u):
                if b is not None:
                    norm1(b)
                if a is not None:
                    normalise_p(a)
                    rsqrt2(a)
                    gate_exp(a)

            schedule(pool, step, prologue)

        @block.scalar
        def _(act):
            def x1_high(a):
                for k, (j0, n) in enumerate(((0, 4), (4, 3))):
                    act.wait_ge(t1_done, at(a, N_T1, k + 1))
                    src = bank[5 + k][0:C, 0:n * LANES].rearrange("p (j h w r) -> p h j w r", h=2, w=NW, r=W)
                    dst = windows(x1_hi[0:C, :])
                    for half in range(2):
                        nc.scalar.activation(dst[:, half, :, j0:j0 + n, :].rearrange("p w j r -> p j w r"),
                                             src[:, half], ACT.Copy).then_inc(x1hi_done, 1)

            def v_copies(a):
                for k in range(2):
                    act.wait_ge(v_done, at(a, N_V, k + 1))
                    for s in range(2):
                        for odd in range(2):
                            nc.scalar.activation(v_dst(k, s, odd), v_src(k, s, odd), ACT.Copy,
                                                 scale=1.0 / WSCALE).then_inc(v_saved, 1)

            def qk_high(a, t):
                kind, half = 1 - t // 2, t % 2
                act.wait_ge(qk_done, at(a, N_QK, t + 1))
                nc.scalar.activation(qk_hi[:, kind, half * STRIP:(half + 1) * STRIP], bank[t % 2][0:C, 0:STRIP],
                                     ACT.Copy, scale=QK_SCALE[kind]).then_inc(qkhi_done, 1)

            def x2_high(f, b):
                for k, (j0, n) in enumerate(((0, 4), (4, 3))):
                    if k == 1 and b is not None:
                        qk_high(b, 3)
                    act.wait_ge(t2_done, at(f, N_T2, k + 1))
                    nc.scalar.activation(x2_hi[0:C, j0 * LANES:(j0 + n) * LANES],
                                         bank[5 + k][0:C, 0:n * LANES], ACT.Copy).then_inc(x2hi_done, 1)

            def load_tables(function):
                nc.scalar.activation(tables[:, :], cst[0:1, 4:5], function)

            def gelus(f, k0):
                for k in range(k0, k0 + 3):
                    chunk, half = hidden_part(k)
                    act.wait_ge(h_done, at(f, N_H, k + 1))
                    nc.scalar.activation(g_sb[:, chunk, half * STRIP:(half + 1) * STRIP],
                                         h_bank[k % 3][:, 0:STRIP], ACT.Gelu,
                                         scale=1.0 / WSCALE).then_inc(gelu_done, 1)

            def exps(a, n):
                act.wait_ge(sub_done, at(a, N_S, n + 1))
                if n >= 2:
                    act.wait_ge(pt_done, at(a, N_PT, 2 * (n - 1)))
                elif not first(a):
                    act.wait_ge(pt_done, at(a, N_PT))
                nc.scalar.activation(p_sb[0:SPAN, n % 2, :, 0:WW], s_sub[:, :, 0:WW], ACT.Exp).then_inc(exp_done, 1)

            def copy_pt(a, n):
                act.wait_ge(pt_done, at(a, N_PT, 2 * n + 2))
                nc.scalar.activation(
                    pt_sb[0:SPAN, :, :].rearrange("p h (s q) -> p h s q", s=2),
                    ps_t[0:SPAN, 0:PAIRS * 128].rearrange("p (h s q) -> p h s q", s=2, q=NB)[:, :, :, 0:WW],
                    ACT.Copy).then_inc(pt_saved, 1)

            def save_o(a, n):
                half, wr = n // 4, 2 * (n % 4)
                act.wait_ge(o_done, at(a, N_O, n + 1))
                if n == 0 and not first(a):
                    act.wait_ge(proj_done, at(a, N_PROJ))
                dst = o_sb[0:C, :, :].rearrange("p b (c h r) -> p b c h r", c=W, h=2)
                nc.scalar.activation(dst[:, :, :, half, W * wr:W * (wr + 2)],
                                     ps_o[0:C, 0:4 * WW].rearrange("p (b c r) -> p b c r", b=2, c=W),
                                     ACT.Copy).then_inc(o_saved, 1)

            def attention(a, b):
                exps(a, 0)
                for n in range(8):
                    if n < 7:
                        exps(a, n + 1)
                    if n == 7 and b is not None:
                        qk_high(b, 0)
                    if n:
                        save_o(a, n - 1)
                    if n == 7 and b is not None:
                        qk_high(b, 1)
                    copy_pt(a, n)
                    if n == T1_AT and b is not None:
                        x1_high(b)
                if b is not None:
                    qk_high(b, 2)
                save_o(a, 7)
                if b is not None:
                    v_copies(b)
                load_tables(ACT.Gelu)
                x2_high(a, b)

            def prologue():
                act.wait_ge(s_ready, 1)
                x1_high((0, 0))
                qk_high((0, 0), 0)
                qk_high((0, 0), 1)
                v_copies((0, 0))
                qk_high((0, 0), 2)
                qk_high((0, 0), 3)
                attention((0, 0), (0, 1))

            def step(f, a, b, u):
                for i in range(8):
                    gelus(f, 3 * i)
                if a is not None:
                    load_tables(ACT.Exp)
                    attention(a, b)

            schedule(act, step, prologue)

        @block.vector
        def _(dve):
            fills = [0]

            def fill(ins):
                fills[0] += 1
                ins.then_inc(s_fill, 1)
                dve.wait_ge(s_fill, fills[0])

            V = nc.vector

            def setup():
                raw = g_sb[:, :, :].rearrange("p a b -> p (a b)")
                offs, o = {}, 0
                for name, n in SETUP:
                    offs[name] = raw[:, o:o + n]
                    o += n
                dve.wait_ge(s_const, 16 * N_CONST)
                dve.wait_ge(s_zero, 3)
                fill(V.tensor_copy(sel16[:, :], offs["sel"]))
                fill(V.tensor_copy(selB16[:, :], offs["selB"]))
                fill(V.tensor_copy(ul16[:, :], offs["ul"]))
                for src, hi, lo in (("wqk", wqk_hi, wqk_lo), ("wv", wv_hi, wv_lo),
                                    ("wg", wg_hi, wg_lo), ("w1", w1_hi, w1_lo)):
                    fill(V.tensor_scalar(hi[:, :], offs[src], WSCALE, None, ALU.mult))
                    fill(V.scalar_tensor_tensor(out=lo[:, :], in0=offs[src], scalar=WSCALE, in1=hi[:, :],
                                                op0=ALU.mult, op1=ALU.subtract))
                tmp = q_st[:, :, :].rearrange("p g t -> p (g t)")[:, 0:B2_COLS]
                fill(V.tensor_copy(tmp, offs["b2"]))
                fill(V.memset(b2_16[:, :], 0.0))
                fill(V.tensor_copy(b2_16[0:1, :], tmp[0:1, :]))
                fill(V.tensor_tensor(b2_16[32:33, :], offs["b2"][32:33, :], tmp[32:33, :], ALU.subtract))
                fill(V.memset(ones16[:, :], 1.0))
                tmp = x1_hi[:, 0:HEADS * WW]
                fill(V.tensor_copy(tmp, offs["rel"]))
                for v in range(2):
                    fill(V.tensor_tensor(bias16[NB:128, v, :], offs["rel"][NB:128, :], tmp[NB:128, :],
                                         ALU.subtract))
                fill(V.tensor_copy(bias16[0:NB, 0, :], tmp[0:NB, :]))
                fill(V.tensor_tensor(bias16[0:NB, 1, :], offs["rel"][0:NB, :], offs["lr"][0:NB, :], ALU.add))
                fill(V.memset(q_st[C:128, :, :], 0.0))
                fill(V.memset(o_sb[C:128, :, :], 0.0))
                fill(V.memset(o_sb[C:C + 1, 0, :], 1.0))
                fill(V.memset(x2_hi[:, :], 0.0))
                fill(V.memset(x2_lo[:, :], 0.0))
                for hi, lo in ((x1_hi, x1_lo), (x2_hi, x2_lo)):
                    fill(V.memset(hi[ONES_ROW:128, :], 0.0))
                    fill(V.memset(hi[ONES_ROW:ONES_ROW + 1, :], 1.0))
                    fill(V.memset(lo[ONES_ROW:128, :], 0.0))
                V.memset(s_sub[:, :, :], 0.0).then_inc(s_ready, 1)
                dve.wait_ge(s_ready, 1)

            def ln1_stats(a):
                u = a[1] % UPI
                per = 16 * len(piece_list(u, SHIFT_IN))
                dve.wait_ge(xa_in[u], a[0] * per + (a[1] // UPI + 1) * per)
                if not first(a):
                    dve.wait_ge(norm1_done, at(a, 1))
                for t in range(W):
                    V.bn_stats(stat1[:, t, :], xa[:, u, t * C:(t + 1) * C]).then_inc(stat1_done, 1)
                dve.wait_ge(stat1_done, at(a, W, W))
                V.memset(mark[:, :], 0.0)
                for t in range(W):
                    V.bn_aggr(mv1[:, t, :], stat1[:, t, :]).then_inc(aggr1_done, 1)
                dve.wait_ge(aggr1_done, at(a, W, W))
                V.tensor_scalar(ve1[:, :], mv1[:, :, 1], EPS_C, None, ALU.add).then_inc(var1_done, 1)

            def x1_low(a, parts=range(4)):
                dst, hi = windows(x1_lo[0:C, :]), windows(x1_hi[0:C, :])
                for k, (j0, n) in enumerate(((0, 4), (4, 3))):
                    src = bank[5 + k][0:C, 0:n * LANES].rearrange("p (j h w r) -> p h j w r", h=2, w=NW, r=W)
                    for half in range(2):
                        if 2 * k + half not in parts:
                            continue
                        dve.wait_ge(x1hi_done, at(a, N_XHI, 2 * k + 2))
                        V.tensor_tensor(dst[:, half, :, j0:j0 + n, :].rearrange("p w j r -> p j w r"),
                                        src[:, half],
                                        hi[:, half, :, j0:j0 + n, :].rearrange("p w j r -> p j w r"),
                                        ALU.subtract).then_inc(x1lo_done, 1)

            def qk_low(a, t):
                kind, half = 1 - t // 2, t % 2
                cols = slice(half * STRIP, (half + 1) * STRIP)
                dve.wait_ge(qkhi_done, at(a, N_QK, t + 1))
                V.scalar_tensor_tensor(out=qk_lo[:, kind, cols], in0=bank[t % 2][0:C, 0:STRIP],
                                       scalar=QK_SCALE[kind], in1=qk_hi[:, kind, cols],
                                       op0=ALU.mult, op1=ALU.subtract).then_inc(qklo_done, 1)

            def spread_keys(a):
                dve.wait_ge(k_in, at(a, N_STACK, N_STACK))
                for g in range(GROUPS):
                    for j in range(GH):
                        V.tensor_scalar(k_bd[0:C, g, j, :], k_st[:, g, :], head_rows[:, j:j + 1], None,
                                        ALU.mult).then_inc(kbd_done, 1)

            def softmax_pair(a, n):
                scores = ps_s[0:SPAN, 0:HEADS * NB].rearrange("p (h k) -> p h k", k=NB)[:, :, 0:WW]
                dve.wait_ge(s_done, at(a, N_S, n + 1))
                V.tensor_reduce(s_max[:, :], scores, AX.X, ALU.max).then_inc(max_done, 1)
                dve.wait_ge(max_done, at(a, N_S, n + 1))
                V.tensor_tensor(s_sub[:, :, 0:WW], scores,
                                s_max[:, :].unsqueeze(2).broadcast_to([SPAN, HEADS, WW]),
                                ALU.subtract).then_inc(sub_done, 1)

            def sums(a, n):
                dve.wait_ge(exp_done, at(a, N_S, n + 1))
                if n or not first(a):
                    dve.wait_ge(pnorm_done, at(a, N_S, n))
                V.tensor_reduce(s_sum[:, :], p_sb[0:SPAN, n % 2, :, 0:WW], AX.X, ALU.add).then_inc(sum_done, 1)
                dve.wait_ge(sum_done, at(a, N_S, n + 1))
                V.reciprocal(s_rec[:, :], s_sum[:, :]).then_inc(rec_done, 1)

            def residual(f):
                u = f[1] % UPI
                per = 16 * len(piece_list(u, SHIFT_OUT))
                rows = xr[:, u, :].rearrange("p (t c) -> p t c", c=C)

                def sums_of(k, j0, n):
                    dve.wait_ge(proj_done, at(f, N_PROJ, k + 1))
                    slot = xr[:, u, j0 * C:(j0 + n) * C]
                    V.tensor_tensor(slot, bank[5 + k][0:LANES, 0:n * C], slot, ALU.add).then_inc(res_done, 1)
                    dve.wait_ge(res_done, at(f, 2, k + 1))
                    for t in range(j0, j0 + n):
                        V.bn_stats(stat2[:, t, :], rows[:, t, :]).then_inc(stat2_done, 1)

                def variances(k, j0, n):
                    dve.wait_ge(stat2_done, at(f, W, j0 + n))
                    V.memset(mark[:, :], 0.0)
                    for t in range(j0, j0 + n):
                        V.bn_aggr(mv2[:, t, :], stat2[:, t, :]).then_inc(aggr2_done, 1)
                    dve.wait_ge(aggr2_done, at(f, W, j0 + n))
                    V.tensor_scalar(ve2[:, j0:j0 + n], mv2[:, j0:j0 + n, 1], EPS_T, None, ALU.add
                                    ).then_inc(var2_done, 1)

                def centre(k, j0, n):
                    V.tensor_tensor(xn2[:, j0:j0 + n, :], rows[:, j0:j0 + n, :],
                                    mv2[:, j0:j0 + n, 0:1].broadcast_to([LANES, n, C]), ALU.subtract
                                    ).then_inc(centre2_done, 1)

                def scale(k, j0, n):
                    dve.wait_ge(centre2_done, at(f, 2, k + 1))
                    dve.wait_ge(rstd2_done, at(f, 2, k + 1))
                    V.tensor_tensor(xn2[:, j0:j0 + n, :], xn2[:, j0:j0 + n, :],
                                    rstd2[:, j0:j0 + n].unsqueeze(2).broadcast_to([LANES, n, C]),
                                    ALU.mult).then_inc(norm2_done, 1)

                dve.wait_ge(xr_in[u], f[0] * per + (f[1] // UPI + 1) * per)
                first_part, second_part = (0, 0, 4), (1, 4, 3)
                sums_of(*first_part)
                variances(*first_part)
                sums_of(*second_part)
                centre(*first_part)
                variances(*second_part)
                scale(*first_part)
                centre(*second_part)
                scale(*second_part)
                x2_low(f, 0)
                x2_low(f, 1)

            def x2_low(f, k):
                j0, n = ((0, 4), (4, 3))[k]
                cols = slice(j0 * LANES, (j0 + n) * LANES)
                dve.wait_ge(x2hi_done, at(f, 2, k + 1))
                V.tensor_tensor(x2_lo[0:C, cols], bank[5 + k][0:C, 0:n * LANES], x2_hi[0:C, cols],
                                ALU.subtract).then_inc(x2lo_done, 1)

            def router_a(f):
                sc = bank[0][0:LANES, 0:W * EXPERTS].rearrange("p (t e) -> p t e", e=EXPERTS)
                dve.wait_ge(gate_done, at(f, 1, 1))
                V.tensor_reduce(gmax[:, :], sc, AX.X, ALU.max).then_inc(router, 1)
                dve.wait_ge(router, at(f, N_ROUTER, 1))
                V.tensor_tensor(gsub[:, :, :], sc, gmax[:, :].unsqueeze(2).broadcast_to([LANES, W, EXPERTS]),
                                ALU.subtract).then_inc(router, 1)
                dve.wait_ge(router, at(f, N_ROUTER, 2))
                V.tensor_scalar(gsub[:, :, :], gsub[:, :, :], 1.0 / WSCALE, None, ALU.mult).then_inc(router, 1)

            def router_b(f):
                k = [3]

                def link(ins):
                    k[0] += 1
                    ins.then_inc(router, 1)
                    dve.wait_ge(router, at(f, N_ROUTER, k[0]))

                ge = gexp[:, :, :]
                mine = ge.rearrange("p t e -> p (t e)").unsqueeze(2).broadcast_to([LANES, W * EXPERTS, EXPERTS])
                mine = mine.rearrange("p (t e) f -> p t e f", e=EXPERTS)
                other = ge.unsqueeze(2).broadcast_to([LANES, W, EXPERTS, EXPERTS])
                gt4 = ggt[:, :, :].rearrange("p (t e) f -> p t e f", e=EXPERTS)
                eq4 = geq[:, :, :].rearrange("p (t e) f -> p t e f", e=EXPERTS)
                dve.wait_ge(gexp_done, at(f, 1, 1))
                V.tensor_tensor(gt4, other, mine, ALU.is_gt).then_inc(router, 1)
                k[0] += 1
                link(V.tensor_tensor(eq4, other, mine, ALU.is_equal))
                link(V.tensor_tensor(eq4, eq4, tie.unsqueeze(1).broadcast_to([LANES, W, EXPERTS, EXPERTS]),
                                     ALU.mult))
                link(V.tensor_tensor(ggt[:, :, :], ggt[:, :, :], geq[:, :, :], ALU.add))
                link(V.tensor_reduce(rank[:, :], ggt[:, :, :], AX.X, ALU.add))
                link(V.scalar_tensor_tensor(out=gsel[:, :, :].rearrange("p t e -> p (t e)"), in0=rank[:, :],
                                            scalar=1.5, in1=ge.rearrange("p t e -> p (t e)"),
                                            op0=ALU.is_lt, op1=ALU.mult))
                V.tensor_reduce(gtot[:, :], ge, AX.X, ALU.add).then_inc(router, 1)
                k[0] += 1
                link(V.tensor_reduce(gden[:, :], gsel[:, :, :], AX.X, ALU.add))
                link(V.scalar_tensor_tensor(out=gden[:, :], in0=gtot[:, :], scalar=1e-9, in1=gden[:, :],
                                            op0=ALU.mult, op1=ALU.add))
                link(V.reciprocal(gden[:, :], gden[:, :]))
                assert k[0] == N_ROUTER
                V.tensor_tensor(gate[:, :].rearrange("p (t e) -> p t e", e=EXPERTS), gsel[:, :, :],
                                gden[:, :].unsqueeze(2).broadcast_to([LANES, W, EXPERTS]),
                                ALU.mult).then_inc(gate_ready, 1)
                dve.wait_ge(gate_ready, at(f, 1, 1))

            def combine(f, u, g):
                dve.wait_ge(y_done, at(f, N_Y, g + 1))
                for k, (j, e) in enumerate(TURNS[g]):
                    i = 3 * g + k
                    slot = xr[:, u, j * C:(j + 1) * C]
                    if g == 8 and k:
                        dve.wait_ge(comb_done, at(f, N_COMB, i))
                    elif i >= 2:
                        dve.wait_ge(comb_done, at(f, N_COMB, i - 1))
                    V.scalar_tensor_tensor(out=slot, in0=y_bank(g)[0:LANES, k * C:(k + 1) * C],
                                           scalar=gate[:, j * EXPERTS + e:j * EXPERTS + e + 1], in1=slot,
                                           op0=ALU.mult, op1=ALU.add).then_inc(comb_done, 1)

            def prologue():
                setup()
                ln1_stats((0, 0))
                x1_low((0, 0))
                ln1_stats((0, 1))
                for t in range(4):
                    qk_low((0, 0), t)
                spread_keys((0, 0))
                softmax_pair((0, 0), 0)
                attention((0, 0), (0, 1))

            def attention(a, b, f=None, u=None):
                for n in range(8):
                    sums(a, n)
                    if n < 7:
                        softmax_pair(a, n + 1)
                    if f is not None:
                        for g in COMBINES_AT[n]:
                            combine(f, u, g)
                    if b is not None:
                        x1_low(b, X1_LOW_AT[n])
                if b is not None:
                    qk_low(b, 0)
                    qk_low(b, 1)
                    c = following(b)
                    if c is not None:
                        ln1_stats(c)
                    qk_low(b, 2)
                residual(a)
                if b is not None:
                    qk_low(b, 3)
                router_a(a)
                if f is not None:
                    combine(f, u, 8)
                    dve.wait_ge(comb_done, at(f, N_COMB, N_COMB))

            def step(f, a, b, u):
                if a is not None:
                    spread_keys(a)
                router_b(f)
                if a is not None:
                    softmax_pair(a, 0)
                    attention(a, b, f, u)
                else:
                    for g in range(N_Y):
                        combine(f, u, g)

            schedule(dve, step, prologue)

        @block.tensor
        def _(pe):
            T = nc.tensor

            def three(outp, lhs_hi, lhs_lo, rhs_hi, rhs_lo, start=True):
                T.matmul(outp, lhs_hi, rhs_hi, start=start, stop=False, skip_group_check=True)
                T.matmul(outp, lhs_hi, rhs_lo, start=False, stop=False, skip_group_check=True)
                return T.matmul(outp, lhs_lo, rhs_hi, start=False, stop=True, skip_group_check=True)

            def transpose1(a):
                pe.wait_ge(norm1_done, at(a, 1, 1))
                for k, (j0, n) in enumerate(((0, 4), (4, 3))):
                    for j in range(n):
                        ins = T.transpose(bank[5 + k][0:C, j * LANES:(j + 1) * LANES], xn1[:, j0 + j, :],
                                          ident[0:LANES, 0:LANES])
                    ins.then_inc(t1_done, 1)

            def values(a, ks=range(2)):
                for k in ks:
                    for w in range(4):
                        for i, (xt, wt) in enumerate(((x1_hi, wv_hi), (x1_hi, wv_lo), (x1_lo, wv_hi))):
                            for s in range(2):
                                x0 = ((k * 4 + w) * 2 + s) * WW
                                ins = T.matmul(bank[2 + k][NB * s:NB * s + WW, w * C:(w + 1) * C],
                                               xt[:, x0:x0 + WW], wt[:, :], start=(i == 0), stop=(i == 2),
                                               skip_group_check=True)
                    ins.then_inc(v_done, 1)

            def qk(a, t):
                kind, half = 1 - t // 2, t % 2
                if t == 0:
                    pe.wait_ge(x1lo_done, at(a, N_X1LO, N_X1LO))
                if t >= 2:
                    pe.wait_ge(qklo_done, at(a, N_QK, t - 1))
                elif not first(a):
                    pe.wait_ge(sub_done, at(a, N_S))
                cols = slice(half * STRIP, (half + 1) * STRIP)
                rows = slice(kind * C, (kind + 1) * C)
                three(bank[t % 2][0:C, 0:STRIP], wqk_hi[:, rows], wqk_lo[:, rows],
                      x1_hi[:, cols], x1_lo[:, cols]).then_inc(qk_done, 1)

            def scores(a, n):
                half, wr = n // 4, 2 * (n % 4)
                if n == 0:
                    pe.wait_ge(q_in, at(a, N_STACK, N_STACK))
                    pe.wait_ge(kbd_done, at(a, N_KBD, N_KBD))
                else:
                    pe.wait_ge(sub_done, at(a, N_S, n))
                variant = 1 if half == 1 and a[1] % UPI == UPI - 1 else 0
                s3 = ps_s[0:SPAN, 0:HEADS * NB].rearrange("p (h k) -> p h k", k=NB)
                for h0, h1 in ((0, 8), (8, 12)):
                    T.matmul(s3[:, h0:h1, 0:WW], sel16[:, :], bias16[:, variant, h0 * WW:h1 * WW],
                             start=True, stop=False, skip_group_check=True)
                    if wr == NW - 2:
                        T.matmul(s3[:, h0:h1, 0:WW], selB16[:, :], ul16[:, h0 * WW:h1 * WW],
                                 start=False, stop=False, skip_group_check=True)
                for s in range(2):
                    x0 = half * STRIP + (wr + s) * WW
                    part = ps_s[NB * s:NB * s + WW, 0:HEADS * NB].rearrange("p (h k) -> p h k", k=NB)
                    for g in range(GROUPS):
                        ins = T.matmul(part[:, g * GH:(g + 1) * GH, 0:WW], q_st[:, g, x0:x0 + WW],
                                       k_bd[:, g, :, x0:x0 + WW],
                                       start=False, stop=True, skip_group_check=True)
                ins.then_inc(s_done, 1)

            def transpose_p(a, n):
                if n == 0:
                    pe.wait_ge(v_saved, at(a, N_XV, N_XV))
                pe.wait_ge(pnorm_done, at(a, N_S, n + 1))
                for p in range(PAIRS):
                    ins = T.transpose(bank[2 + p // 4][0:SPAN, (p % 4) * 128:(p % 4) * 128 + SPAN],
                                      p_sb[0:SPAN, n % 2, 2 * p:2 * p + 2, :].rearrange("p h k -> p (h k)")[:, 0:SPAN],
                                      ident[0:SPAN, 0:SPAN])
                    if p in (3, 5):
                        ins.then_inc(pt_done, 1)

            def attend(a, n):
                half, wr = n // 4, 2 * (n % 4)
                pe.wait_ge(pt_saved, at(a, N_S, n + 1))
                if n:
                    pe.wait_ge(o_saved, at(a, N_O, n))
                for s in range(2):
                    win = half * NW + wr + s
                    for p in range(PAIRS):
                        rows = slice(32 * (p % 3), 32 * (p % 3) + 32)
                        o = ps_o[rows, (p // 3) * 98:(p // 3) * 98 + 98]
                        o = o.rearrange("p (c s r) -> p c s r", c=W, s=2)[:, :, s, :]
                        ins = T.matmul(o, v_bd[0:SPAN, win * PAIRS + p, :], pt_sb[0:SPAN, p, s * WW:(s + 1) * WW],
                                       start=True, stop=True, skip_group_check=True)
                ins.then_inc(o_done, 1)

            def project(f):
                pe.wait_ge(o_saved, at(f, N_O, N_O))
                for k, (j0, n) in enumerate(((0, 4), (4, 3))):
                    for j in range(n):
                        for blk in range(2):
                            ins = T.matmul(bank[5 + k][0:LANES, j * C:(j + 1) * C],
                                           o_sb[:, blk, (j0 + j) * LANES:(j0 + j + 1) * LANES],
                                           wp_sb[:, blk, :], start=(blk == 0), stop=(blk == 1))
                    ins.then_inc(proj_done, 1)

            def transpose2(f, b):
                for k, (j0, n) in enumerate(((0, 4), (4, 3))):
                    if k == 1 and b is not None:
                        qk(b, 3)
                    pe.wait_ge(norm2_done, at(f, 2, k + 1))
                    for j in range(n):
                        ins = T.transpose(bank[5 + k][0:C, j * LANES:(j + 1) * LANES], xn2[:, j0 + j, :],
                                          ident[0:LANES, 0:LANES])
                    ins.then_inc(t2_done, 1)

            def gate_scores(f):
                pe.wait_ge(x2lo_done, at(f, 2, 2))
                for j in range(W):
                    cols = slice(j * LANES, j * LANES + 128)
                    ins = three(bank[0][:, j * EXPERTS:(j + 1) * EXPERTS], x2_hi[:, cols],
                                x2_lo[:, cols], wg_hi[:, :], wg_lo[:, :])
                ins.then_inc(gate_done, 1)

            def hidden(f, ks):
                for k in ks:
                    chunk, half = hidden_part(k)
                    if k == 0:
                        pe.wait_ge(x2lo_done, at(f, 2, 1))
                    elif k >= 3:
                        pe.wait_ge(gelu_done, at(f, N_H, k - 2))
                    wc = slice(chunk * 128, (chunk + 1) * 128)
                    xc = slice(half * STRIP, (half + 1) * STRIP)
                    three(h_bank[k % 3][:, 0:STRIP], w1_hi[:, wc], w1_lo[:, wc],
                          x2_hi[:, xc], x2_lo[:, xc]).then_inc(h_done, 1)

            def experts(f, g):
                if g == 0:
                    pe.wait_ge(gelu_done, at(f, N_H, N_H - 2))
                elif g == 1:
                    pe.wait_ge(gelu_done, at(f, N_H, N_H - 1))
                elif g == 2:
                    pe.wait_ge(gelu_done, at(f, N_H, N_H))
                elif g < 8:
                    before = max(i for i in range(g) if Y_BANK[i] == Y_BANK[g])
                    pe.wait_ge(comb_done, at(f, N_COMB, 3 * before + 3))
                n = len(TURNS[g])
                y = y_bank(g)[0:LANES, 0:n * C]
                if n == 3:
                    b0 = 3 * g % (2 * EXPERTS) * C
                    bias = b2_16[:, b0:b0 + n * C]
                else:
                    bias = b2_16[:, 0:2 * n * C].rearrange("p (e s c) -> p e s c", s=2, c=C)[:, :, 0, :]
                T.matmul(y, ones16[:, :], bias, start=True, stop=False, skip_group_check=True)
                for k, (j, e) in enumerate(TURNS[g]):
                    for c in range(CPE):
                        ins = T.matmul(y[:, k * C:(k + 1) * C],
                                       g_sb[:, e * CPE + c, j * LANES:(j + 1) * LANES],
                                       w2_sb[:, e * CPE + c, :], start=False, stop=(c == CPE - 1),
                                       skip_group_check=True)
                ins.then_inc(y_done, 1)

            def prologue():
                pe.wait_ge(s_ready, 1)
                transpose1((0, 0))
                for t in range(4):
                    qk((0, 0), t)
                    if t == 1:
                        values((0, 0))
                scores((0, 0), 0)
                attention((0, 0), (0, 1))

            def attention(a, b, f=None):
                for n in range(9):
                    groups = list(GROUPS_AT[n]) if f is not None else []
                    if n == 0 and groups:
                        experts(f, groups.pop(0))
                    if n < 7:
                        scores(a, n + 1)
                    for g in groups:
                        experts(f, g)
                    if n == T1_AT and b is not None:
                        if f is not None:
                            pe.wait_ge(comb_done, at(f, N_COMB, 15))
                        transpose1(b)
                    if n >= 7 and b is not None:
                        qk(b, 2 * (n - 7))
                    if n:
                        attend(a, n - 1)
                    if n == 7 and b is not None:
                        qk(b, 1)
                    if n < 8:
                        transpose_p(a, n)
                if b is not None:
                    values(b, (0,))
                project(a)
                if b is not None:
                    values(b, (1,))
                if f is not None:
                    experts(f, 8)
                transpose2(a, b)
                hidden(a, (0, 1))
                gate_scores(a)

            def step(f, a, b, u):
                for i in range(8):
                    hidden(f, range(max(2, 3 * i), 3 * i + 3))
                if a is not None:
                    scores(a, 0)
                if a is not None:
                    attention(a, b, f)
                else:
                    for g in range(N_Y):
                        experts(f, g)

            schedule(pe, step, prologue)


def _rows(a, rows=128):
    out = np.zeros((rows,) + a.shape[1:], a.dtype)
    out[:a.shape[0]] = a
    return out


def _layout(w_qkv, b_qkv, w_proj, b_proj, rel_table, gate_w, gate_b, w1, b1, w2, b2):
    f = np.float32
    wb = np.concatenate([w_qkv.T, b_qkv[None]], 0)
    wqk = wb[:, :2 * C]
    wv = wb[:, 2 * C:].reshape(97, PAIRS, 2, HD).transpose(0, 2, 1, 3).reshape(97, C)
    wg = np.concatenate([gate_w, gate_b[None]], 0)
    w1b = np.concatenate([w1.transpose(1, 0, 2).reshape(C, EXPERTS * HID), b1.reshape(1, -1)], 0)
    b2r = np.zeros((128, B2_COLS), f)
    b2r[0] = b2r[32] = np.concatenate([np.repeat(b2, 2, 0), b2[:1], b2[:1]]).reshape(-1)
    col, row = np.arange(WW) // W, np.arange(WW) % W
    idx = (row[:, None] - row[None] + W - 1) * (2 * W - 1) + (col[:, None] - col[None] + W - 1)
    rel = np.zeros((128, HEADS, WW), f)
    rel[0:WW] = rel[NB:SPAN] = rel_table[idx].transpose(0, 2, 1)
    late = lambda v: v >= W - W // 2
    lr, ul = np.zeros((128, HEADS, WW), f), np.zeros((128, HEADS, WW), f)
    lr[0:WW] = np.where(late(col)[:, None] != late(col)[None], MASKED, 0.0)[:, None, :]
    ul[0:WW] = np.where(late(row)[:, None] != late(row)[None], MASKED, 0.0)[:, None, :]
    sel, selB = np.zeros((128, SPAN), f), np.zeros((128, SPAN), f)
    q = np.arange(WW)
    for k0 in (0, NB):
        for m0 in (0, NB):
            sel[k0 + q, m0 + q] = 1.0
    selB[q, NB + q] = 1.0
    parts = {"wqk": _rows(wqk), "wv": _rows(wv), "wg": _rows(wg), "w1": _rows(w1b), "b2": b2r,
             "rel": rel.reshape(128, -1), "lr": lr.reshape(128, -1), "ul": ul.reshape(128, -1),
             "sel": sel, "selB": selB}
    packed = np.concatenate([parts[name] for name, _ in SETUP], 1).astype(f)
    wp = np.zeros((2, 128, C), f)
    wp[:, 0:C].reshape(2, 3, 32, C)[:, :, 0:16] = w_proj.T.reshape(2, 3, 16, C)
    wp[0, C] = b_proj
    wp = np.ascontiguousarray(wp.transpose(1, 0, 2))
    w2p = np.ascontiguousarray(w2.reshape(EXPERTS, CPE, 128, C).transpose(2, 0, 1, 3).reshape(128, CHUNKS, C))
    consts = np.zeros((128, 150), f)
    consts[:, 0:128] = np.eye(128)
    row_head = np.arange(128) % 32 // HD
    consts[:, 128:132] = row_head[:, None] == np.arange(GH)
    consts[:, 132] = -0.5
    consts[:, 133] = np.e
    e = np.arange(EXPERTS)
    consts[:, 134:150] = (e[None, :] < e[:, None]).astype(f).reshape(1, -1)
    return packed, w2p, wp, consts


def kernel(**inputs):
    import concourse.bacc as bacc
    from concourse.bass_utils import run_bass_kernel_spmd

    a = {k: np.asarray(v) for k, v in inputs.items()}
    c, g = "L0_conv_", "L0_ffn_"
    packed, w2, wp, consts = _layout(a[c + "w_qkv"], a[c + "b_qkv"], a[c + "w_proj"], a[c + "b_proj"],
                                     a[c + "rel_table"], a[g + "gate_w"], a[g + "gate_b"],
                                     a[g + "w1"], a[g + "b1"], a[g + "w2"], a[g + "b2"])
    arrays = {"x": np.ascontiguousarray(a["x"]).reshape(B, IMG, IMG * C), "packed": packed, "w2": w2,
              "wp": wp, "consts": consts}
    nc = bacc.Bacc("TRN2", target_bir_lowering=False, num_devices=1)
    aps = [nc.dram_tensor(n, v.shape, F32, kind="ExternalInput").ap() for n, v in arrays.items()]
    out = nc.dram_tensor("out", (B, IMG, IMG * C), F32, kind="ExternalOutput").ap()
    build(nc, *aps, out)
    r = run_bass_kernel_spmd(nc, [arrays], core_ids=[0])
    return r.results[0]["out"].reshape(B, IMG, IMG, C)
```
